# Optimizing a Trainium2 kernel written in Bass

```python
import numpy as np
import jax
import jax.numpy as jnp

def _softmax(x, axis=-1):
    return jax.nn.softmax(x, axis=axis)

def _gelu(x):
    return jax.nn.gelu(x, approximate=True)

def _silu(x):
    return jax.nn.silu(x)

def _sigmoid(x):
    return jax.nn.sigmoid(x)

def _layernorm(x, axis=-1, eps=1e-05):
    m = jnp.mean(x, axis=axis, keepdims=True)
    v = jnp.var(x, axis=axis, keepdims=True)
    return (x - m) / jnp.sqrt(v + eps)

def _scatter_add(tgt, idx, src, axis=0):
    return tgt.at[idx].add(src)

def _segment_sum(src, seg, n):
    return jax.ops.segment_sum(src, seg, n)
kernel_name = 'mk_flamingo_gated_d1_seqx_r4_573a83'

def setup_inputs(seed: int=0):
    np.random.seed(seed)
    _w = jnp.asarray

    def _rec_inputs():
        import jax
        import jax.numpy as jnp
        _rk = jax.random.key(seed)
        x = -0.0002928 + 1 * jax.random.normal(jax.random.fold_in(_rk, 1), (16, 128, 256), jnp.float32)
        _lenS = 128 - jax.random.randint(jax.random.fold_in(_rk, 7), (16,), 0, max(1, 128 // 4) + 1, jnp.int32)
        _lenS2 = 128 - jax.random.randint(jax.random.fold_in(_rk, 8), (16,), 0, max(1, 128 // 4) + 1, jnp.int32)
        _ctx_1024P = jax.random.normal(jax.random.fold_in(_rk, 11), (16, 16, 256), jnp.float32)
        _ctx_1024c = jax.random.dirichlet(jax.random.fold_in(_rk, 511), 0.3 * jnp.ones((16,), jnp.float32), (16, 128))
        _ctx_1024t = jnp.einsum('bsk,bkd->bsd', _ctx_1024c, _ctx_1024P)
        _ctx_1024t = _ctx_1024t * jax.lax.rsqrt(jnp.mean(jnp.square(_ctx_1024t)) + 1e-12) * 0.953939
        ctx_1024 = -1.39393e-06 + 0.999914 * (_ctx_1024t + 0.3 * jax.random.normal(jax.random.fold_in(_rk, 611), (16, 128, 256), jnp.float32))
        _g = jax.random.normal(jax.random.fold_in(_rk, 9001), (2, 1), jnp.float32)
        _g = jnp.sign(_g) * jnp.maximum(jnp.abs(_g), 1.0) + (_g == 0) * 1.0
        g_xattn = _g[0]
        g_ffn = _g[1]
        return (x, ctx_1024, g_xattn, g_ffn)
    x, ctx_1024, g_xattn, g_ffn = _rec_inputs()

    def _L0_xattn_setup():
        import jax, jax.numpy as jnp
        import numpy as np
        D_MODEL = 256
        NHEAD = 16
        D_HEAD = D_MODEL // NHEAD
        B, L = (2, 512)
        key = jax.random.key(seed)
        ks = jax.random.split(key, 11)
        s = 1.0 / np.sqrt(D_MODEL)
        return {'Q': jax.random.normal(ks[0], (B, L, D_MODEL), jnp.float32), 'K': jax.random.normal(ks[1], (B, L, D_MODEL), jnp.float32), 'V': jax.random.normal(ks[2], (B, L, D_MODEL), jnp.float32), 'Wq': jax.random.normal(ks[3], (D_MODEL, D_MODEL), jnp.float32) * s, 'bq': jax.random.normal(ks[4], (D_MODEL,), jnp.float32) * 0.01, 'Wk': jax.random.normal(ks[5], (D_MODEL, D_MODEL), jnp.float32) * s, 'bk': jax.random.normal(ks[6], (D_MODEL,), jnp.float32) * 0.01, 'Wv': jax.random.normal(ks[7], (D_MODEL, D_MODEL), jnp.float32) * s, 'bv': jax.random.normal(ks[8], (D_MODEL,), jnp.float32) * 0.01, 'Wo': jax.random.normal(ks[9], (D_MODEL, D_MODEL), jnp.float32) * s, 'bo': jax.random.normal(ks[10], (D_MODEL,), jnp.float32) * 0.01}
    _L0_xattn_all = _L0_xattn_setup()
    _L0_xattn_in = {k: v for k, v in _L0_xattn_all.items() if k in ('Wq', 'bq', 'Wk', 'bk', 'Wv', 'bv', 'Wo', 'bo')}
    del _L0_xattn_all

    def _L0_ffn_setup():
        import jax, jax.numpy as jnp
        import numpy as np
        B, T, D = (2, 256, 256)
        E = 16
        H = 512
        K = 2
        HS = H * 2
        key = jax.random.key(seed)
        ks = jax.random.split(key, 16)
        s = 0.02
        f32 = jnp.float32
        return {'x': jax.random.normal(ks[0], (B, T, D), f32), 'Wg': jax.random.normal(ks[1], (D, E), f32) * s, 'W1': jax.random.normal(ks[2], (E, D, H), f32) * s, 'b1': jax.random.normal(ks[3], (E, H), f32) * s, 'W11': jax.random.normal(ks[4], (E, D, H), f32) * s, 'b11': jax.random.normal(ks[5], (E, H), f32) * s, 'W2': jax.random.normal(ks[6], (E, H, D), f32) * s, 'b2': jax.random.normal(ks[7], (E, D), f32) * s, 'Ws1': jax.random.normal(ks[8], (D, HS), f32) * s, 'bs1': jax.random.normal(ks[9], (HS,), f32) * s, 'Ws11': jax.random.normal(ks[10], (D, HS), f32) * s, 'bs11': jax.random.normal(ks[11], (HS,), f32) * s, 'Ws2': jax.random.normal(ks[12], (HS, D), f32) * s, 'bs2': jax.random.normal(ks[13], (D,), f32) * s}
    _L0_ffn_all = _L0_ffn_setup()
    _L0_ffn_in = {k: v for k, v in _L0_ffn_all.items() if k in ('Wg', 'W1', 'b1', 'W11', 'b11', 'W2', 'b2', 'Ws1', 'bs1', 'Ws11', 'bs11', 'Ws2', 'bs2')}
    del _L0_ffn_all
    return {'x': x, 'ctx_1024': ctx_1024, 'g_xattn': g_xattn, 'g_ffn': g_ffn, 'L0_xattn_Wq': _L0_xattn_in['Wq'], 'L0_xattn_bq': _L0_xattn_in['bq'], 'L0_xattn_Wk': _L0_xattn_in['Wk'], 'L0_xattn_bk': _L0_xattn_in['bk'], 'L0_xattn_Wv': _L0_xattn_in['Wv'], 'L0_xattn_bv': _L0_xattn_in['bv'], 'L0_xattn_Wo': _L0_xattn_in['Wo'], 'L0_xattn_bo': _L0_xattn_in['bo'], 'L0_ffn_Wg': _L0_ffn_in['Wg'], 'L0_ffn_W1': _L0_ffn_in['W1'], 'L0_ffn_b1': _L0_ffn_in['b1'], 'L0_ffn_W11': _L0_ffn_in['W11'], 'L0_ffn_b11': _L0_ffn_in['b11'], 'L0_ffn_W2': _L0_ffn_in['W2'], 'L0_ffn_b2': _L0_ffn_in['b2'], 'L0_ffn_Ws1': _L0_ffn_in['Ws1'], 'L0_ffn_bs1': _L0_ffn_in['bs1'], 'L0_ffn_Ws11': _L0_ffn_in['Ws11'], 'L0_ffn_bs11': _L0_ffn_in['bs11'], 'L0_ffn_Ws2': _L0_ffn_in['Ws2'], 'L0_ffn_bs2': _L0_ffn_in['bs2']}

def reference(x, ctx_1024, g_xattn, g_ffn, L0_xattn_Wq, L0_xattn_bq, L0_xattn_Wk, L0_xattn_bk, L0_xattn_Wv, L0_xattn_bv, L0_xattn_Wo, L0_xattn_bo, L0_ffn_Wg, L0_ffn_W1, L0_ffn_b1, L0_ffn_W11, L0_ffn_b11, L0_ffn_W2, L0_ffn_b2, L0_ffn_Ws1, L0_ffn_bs1, L0_ffn_Ws11, L0_ffn_bs11, L0_ffn_Ws2, L0_ffn_bs2):
    import jax
    import jax.numpy as jnp

    def _L0_xattn_ref(Q, K, V, Wq, bq, Wk, bk, Wv, bv, Wo, bo):
        import jax, jax.numpy as jnp
        import numpy as np
        D_MODEL = 256
        NHEAD = 16
        D_HEAD = D_MODEL // NHEAD
        B, L = (2, 512)
        b, l, _ = Q.shape
        q = (Q @ Wq.T + bq).reshape(b, l, NHEAD, D_HEAD)
        k = (K @ Wk.T + bk).reshape(b, l, NHEAD, D_HEAD)
        v = (V @ Wv.T + bv).reshape(b, l, NHEAD, D_HEAD)
        scale = jnp.asarray(1.0 / np.sqrt(D_HEAD), q.dtype)
        scores = jnp.einsum('bqhd,bkhd->bhqk', q, k) * scale
        attn = jax.nn.softmax(scores, axis=-1)
        out = jnp.einsum('bhqk,bkhd->bqhd', attn, v)
        out = out.reshape(b, l, D_MODEL)
        return out @ Wo.T + bo

    def _L0_ffn_ref(x, Wg, W1, b1, W11, b11, W2, b2, Ws1, bs1, Ws11, bs11, Ws2, bs2):
        import jax, jax.numpy as jnp
        import numpy as np
        B, T, D = (2, 256, 256)
        E = 16
        H = 512
        K = 2
        HS = H * 2
        b, t, d = x.shape
        xf = x.reshape(b * t, d)
        n = xf.shape[0]
        logits = xf @ Wg
        _, topi = jax.lax.top_k(logits, K)
        mask = jnp.zeros((n, E), bool).at[jnp.arange(n)[:, None], topi].set(True)
        gates = jax.nn.softmax(jnp.where(mask, logits, -jnp.inf), axis=-1)
        y = jnp.zeros_like(xf)
        for e in range(E):
            h = jax.nn.silu(xf @ W1[e] + b1[e]) * (xf @ W11[e] + b11[e])
            y = y + (h @ W2[e] + b2[e]) * gates[:, e, None]
        z = jax.nn.silu(xf @ Ws1 + bs1) * (xf @ Ws11 + bs11) @ Ws2 + bs2
        return (y + z).reshape(b, t, d)
    x = x + jnp.tanh(g_xattn[0]) * _L0_xattn_ref(_layernorm(x, axis=-1), ctx_1024, ctx_1024, L0_xattn_Wq, L0_xattn_bq, L0_xattn_Wk, L0_xattn_bk, L0_xattn_Wv, L0_xattn_bv, L0_xattn_Wo, L0_xattn_bo)
    x = x + jnp.tanh(g_ffn[0]) * _L0_ffn_ref(_layernorm(x, axis=-1), L0_ffn_Wg, L0_ffn_W1, L0_ffn_b1, L0_ffn_W11, L0_ffn_b11, L0_ffn_W2, L0_ffn_b2, L0_ffn_Ws1, L0_ffn_bs1, L0_ffn_Ws11, L0_ffn_bs11, L0_ffn_Ws2, L0_ffn_bs2)
    return x

_drawn_inputs = setup_inputs


def setup_inputs(seed=0):
    import zlib

    import numpy as np

    out = dict(_drawn_inputs(seed))
    spreads = {}
    factors = {'L0_xattn_bq': 8.0,
     'L0_xattn_bk': 64.0,
     'L0_xattn_bv': 8.0,
     'L0_xattn_bo': 7.651,
     'L0_ffn_Wg': 3.183,
     'L0_ffn_W1': 3.88,
     'L0_ffn_b1': 8.0,
     'L0_ffn_W11': 3.843,
     'L0_ffn_b11': 8.0,
     'L0_ffn_W2': 3.826,
     'L0_ffn_b2': 4.583,
     'L0_ffn_bs1': 39.689,
     'L0_ffn_bs11': 39.864,
     'L0_ffn_bs2': 3.114}
    for name, (base, spread) in spreads.items():
        noise = np.random.default_rng([zlib.crc32(name.encode()), seed]).standard_normal(out[name].shape)
        drawn = base * np.exp(spread * noise) if base else spread * noise
        out[name] = jnp.asarray(drawn.astype(out[name].dtype))
    for name, factor in factors.items():
        out[name] = (out[name] * factor).astype(out[name].dtype)
    return out
```

```python
from contextlib import ExitStack

import concourse.bass as bass
from concourse import mybir

P = 128
F32 = mybir.dt.float32
I32 = mybir.dt.int32
U32 = mybir.dt.uint32
ALU = mybir.AluOpType
ACT = mybir.ActivationFunctionType
AX = mybir.AxisListType

TILES = 16
D = 256
DC = D // P
CTX = 128
NH = 16
DH = D // NH
HG = P // DH
E = 16
HID = 512
HC = HID // P
SHID = 1024
SC = SHID // P
EPS = 1e-5
SCALE = DH ** -0.5
PAIRS = TILES // 2
UNITS = 4
TOKENS = TILES * P
TOPK = 2
BLOCKS = (TOPK * TOKENS + E * (P - 1)) // P
ROWS = BLOCKS * P
LOOPED = (BLOCKS - 4) // 2 * 2
WSLOTS = 3
WCOLS = 2 * DC * HID + HC * D
BCOLS = 2 * HID + D
ZROWS = WCOLS // D
ZDMAS = -(-BLOCKS // ZROWS)
GROUP = 4
GATHERS = 8

C_ID, C_TRI, C_ONE, C_HM = 0, P, 2 * P, 3 * P
C_IE = C_HM + HG
C_IB = C_IE + E
C_IT = C_IB + BLOCKS
CONSTS = C_IT + TILES
B_Q, B_K, B_V, B_S1, B_S11 = 0, DC, 2 * DC, 3 * DC, 3 * DC + SC
BIASES = 3 * DC + 2 * SC


def flamingo_layer(nc, x, ctx_t, attn_w, col_bias, bo, g_xattn, g_ffn, w_gate, experts, expert_bias,
                   shared_w, bs2, consts, out):
    es = ExitStack()
    with es:
        def sb(name, shape, dt=F32):
            return es.enter_context(nc.sbuf_tensor(name, shape, dt))

        def sem(name):
            return es.enter_context(nc.semaphore(name))

        sorted_x = nc.dram_tensor("sorted_x", (ROWS, D), F32, kind="Internal").ap()
        sorted_y = nc.dram_tensor("sorted_y", (ROWS, D), F32, kind="Internal").ap()

        big = es.enter_context(nc.psum_tensor("big", [P, 2, 2, 512], F32))
        mid = es.enter_context(nc.psum_tensor("mid", [P, 2, 512], F32))
        work = es.enter_context(nc.psum_tensor("work", [P, 512], F32))
        last = es.enter_context(nc.psum_tensor("last", [P, 512], F32))

        zbank = (last, work)

        const = sb("const", [P, CONSTS])
        ident = const[:, C_ID:C_ID + P]
        bias = sb("bias", [P, BIASES])
        tanh_g = sb("tanh_g", [P, 2])
        gates_in = sb("gates_in", [P, 2])
        x_all = sb("x_all", [P, TILES, D])
        xf_all = sb("xf_all", [P, TILES, D])
        xfT_all = sb("xfT_all", [P, DC, TOKENS])
        bs2_bc = sb("bs2_bc", [P, D])
        shared = sb("shared", [P, 2 * DC * SHID + SC * D])
        ws1 = shared[:, 0:DC * SHID].rearrange("p (c n) -> p c n", c=DC)
        ws11 = shared[:, DC * SHID:2 * DC * SHID].rearrange("p (c n) -> p c n", c=DC)
        ws2 = shared[:, 2 * DC * SHID:].rearrange("p (c n) -> p c n", c=SC)
        ring = sb("ring", [P, WSLOTS, WCOLS])
        bring = sb("bring", [P, WSLOTS, BCOLS])

        logits = sb("logits", [P, 2, E])
        top8 = sb("top8", [P, 2, 8])
        idx8 = sb("idx8", [P, 2, 8], U32)
        idxf = sb("idxf", [P, 2, 2])
        chosen = sb("chosen", [P, TOPK, TILES, E])
        top2 = sb("top2", [P, TOPK, TILES])
        cnt = sb("cnt", [P, 6, E])
        pos_f = sb("pos_f", [P, TOPK, TILES])
        pos = sb("pos", [P, TOPK, TILES], U32)
        gate = sb("gate", [P, TOPK, TILES])
        gtmp = sb("gtmp", [P, 3, TILES])
        blk_f = sb("blk_f", [P, BLOCKS])
        blk_expert = sb("blk_expert", [P, BLOCKS], I32)
        blk_end = sb("blk_end", [P, E], I32)

        ARENA = 17920
        arena = sb("arena", [P, ARENA])
        taken = [0]

        def part(cols):
            taken[0] += cols
            assert taken[0] <= ARENA, taken[0]
            return arena[:, taken[0] - cols:taken[0]]

        wqkvo = part(4 * DC * D).rearrange("p (w c n) -> p w c n", w=4, c=DC)
        kblk = part(2 * HG * CTX).rearrange("p (s h k) -> p s h k", s=2, h=HG)
        probs = part(2 * HG * CTX).rearrange("p (s h k) -> p s h k", s=2, h=HG)
        pT = part(2 * 4 * P).rearrange("p (g h q) -> p g h q", g=2, h=4)
        VB = HG * (P + DH)
        vmask = part(4 * VB).rearrange("p (u c) -> p u c", u=UNITS)
        xn = part(2 * D).rearrange("p (b n) -> p b n", b=2)
        xnT = part(DC * 2 * P).rearrange("p (c n) -> p c n", c=DC)
        ctxT = part(DC * 2 * CTX).rearrange("p (c n) -> p c n", c=DC)
        qT = part(DC * 2 * P).rearrange("p (c n) -> p c n", c=DC)
        kT = part(DC * 2 * CTX).rearrange("p (c n) -> p c n", c=DC)
        outT = part(UNITS * P).rearrange("p (u q) -> p u q", u=UNITS)
        bo_bc = part(D)
        taken[0] = 0
        gshT = part(SC * 512).rearrange("p (c n) -> p c n", c=SC)
        sil = part(2 * 512).rearrange("p (s n) -> p s n", s=2)
        hb1 = part(2 * HID).rearrange("p (s n) -> p s n", s=2)
        hb11 = part(2 * HID).rearrange("p (s n) -> p s n", s=2)
        sl = part(2 * HID).rearrange("p (s n) -> p s n", s=2)
        gg = part(2 * HID).rearrange("p (s n) -> p s n", s=2)
        gT = part(2 * HID).rearrange("p (s c n) -> p s c n", s=2, c=HC)
        xs = part(2 * D).rearrange("p (s n) -> p s n", s=2)
        xsT = part(2 * D).rearrange("p (s c n) -> p s c n", s=2, c=DC)
        ysb = part(2 * D).rearrange("p (s n) -> p s n", s=2)
        zt = part(D)
        rt = part(4 * TILES * E).rearrange("p (i n) -> p i n", i=4)
        blk_cmp = part(BLOCKS * E).rearrange("p (b e) -> p b e", e=E)
        yg = part(GATHERS * TOPK * D).rearrange("p (t k n) -> p t k n", t=GATHERS, k=TOPK)

        xfs = sb("xfs", [P, 2, D])
        xfT = sb("xfT", [P, DC, 2 * P])
        wg_pad = sb("wg_pad", [P, DC, P])
        stats = sb("stats", [P, 2, 6])
        mv1 = sb("mv1", [P, 2, 2])
        mv2 = sb("mv2", [P, 2, 2])
        ve1 = sb("ve1", [P, 2])
        ve2 = sb("ve2", [P, 2])
        rs1 = sb("rs1", [P, 2])
        rs2 = sb("rs2", [P, 2])
        mhalf = sb("mhalf", [P, 1])
        carrier = sb("carrier", [P, 1])
        rmax = sb("rmax", [P, 2, HG])
        nmax = sb("nmax", [P, 2, HG])
        rsum = sb("rsum", [P, 2, HG])
        rinv = sb("rinv", [P, 2, HG])
        att = sb("att", [P, D])

        gT_ready = sem("gT_ready")
        kT_ready = sem("kT_ready")
        qT_ready = sem("qT_ready")
        xfT_kept = sem("xfT_kept")
        xfT_ps = sem("xfT_ps")
        xfT_ready = sem("xfT_ready")
        xnT_ps = sem("xnT_ps")
        xnT_ready = sem("xnT_ready")
        xsT_ready = sem("xsT_ready")
        const_loaded = sem("const_loaded")
        bias_loaded = sem("bias_loaded")
        x_head_loaded = sem("x_head_loaded")
        x_loaded = sem("x_loaded")
        ctx_loaded = sem("ctx_loaded")
        attn_w_loaded = sem("attn_w_loaded")
        gate_in_loaded = sem("gate_in_loaded")
        wg_loaded = sem("wg_loaded")
        bo_loaded = sem("bo_loaded")
        shared_loaded = sem("shared_loaded")
        zeroed = sem("zeroed")
        tanh_ready = sem("tanh_ready")
        wg_zero = sem("wg_zero")
        half_ready = sem("half_ready")
        vmask_zero = sem("vmask_zero")
        xs_zero = sem("xs_zero")
        dve_step = sem("dve_step")
        ln1_var = sem("ln1_var")
        ln1_rstd = sem("ln1_rstd")
        ln2_var = sem("ln2_var")
        ln2_rstd = sem("ln2_rstd")
        xn_ready = sem("xn_ready")
        k_ps = sem("k_ps")
        q_ps = sem("q_ps")
        v_ps = sem("v_ps")
        v_ready = sem("v_ready")
        kblk_ready = sem("kblk_ready")
        scores_ready = sem("scores_ready")
        negmax_ready = sem("negmax_ready")
        exps_done = sem("exps_done")
        rinv_ready = sem("rinv_ready")
        probs_ready = sem("probs_ready")
        pt_ready = sem("pt_ready")
        pt_copied = sem("pt_copied")
        av_ready = sem("av_ready")
        heads_copied = sem("heads_copied")
        o_ps = sem("o_ps")
        o_taken = sem("o_taken")
        xf_ready = sem("xf_ready")
        xf_kept = sem("xf_kept")
        lg_ps = sem("lg_ps")
        lg_taken = sem("lg_taken")
        onehots_ready = sem("onehots_ready")
        rank_ps = sem("rank_ps")
        rank_taken = sem("rank_taken")
        table_ready = sem("table_ready")
        pos_ready = sem("pos_ready")
        gate_exp_in = sem("gate_exp_in")
        gate_exp = sem("gate_exp")
        scattered = sem("scattered")
        w_even = sem("w_even")
        w_odd = sem("w_odd")
        xs_even = sem("xs_even")
        xs_odd = sem("xs_odd")
        xs_ps = sem("xs_ps")
        up_ps = sem("up_ps")
        h1_ready = sem("h1_ready")
        h_taken = sem("h_taken")
        s_ready = sem("s_ready")
        g_ready = sem("g_ready")
        gt_ps = sem("gt_ps")
        down_ps = sem("down_ps")
        y_ready = sem("y_ready")
        y_st_even = sem("y_st_even")
        y_st_odd = sem("y_st_odd")
        sh_ps = sem("sh_ps")
        silu_ready = sem("silu_ready")
        gsh_ready = sem("gsh_ready")
        z_ps = sem("z_ps")
        z_taken = sem("z_taken")
        z_added = sem("z_added")
        gathered = sem("gathered")
        gathered_b = sem("gathered_b")
        combined = sem("combined")
        gates_ready = sem("gates_ready")
        stored = sem("stored")

        block = es.enter_context(nc.Block())
        N_SH = 2 * SC
        LAST = PAIRS - 1

        @block.sync
        def _(sp):
            sp.dma_start(x_all[:, 0:4, :], x[:, 0:4, :]).then_inc(x_head_loaded, 16)
            sp.dma_start(const[:, :], consts).then_inc(const_loaded, 16)
            sp.dma_start(ctxT, ctx_t[0]).then_inc(ctx_loaded, 16)
            sp.dma_start(wqkvo, attn_w).then_inc(attn_w_loaded, 16)
            sp.dma_start(bias[:, :], col_bias).then_inc(bias_loaded, 16)
            sp.dma_start(x_all[:, 4:TILES, :], x[:, 4:TILES, :]).then_inc(x_loaded, 16)
            sp.dma_start(bo_bc, bo.partition_broadcast(P)).then_inc(bo_loaded, 16)
            sp.dma_start(gates_in[:, 0:1], g_xattn.partition_broadcast(P)).then_inc(gate_in_loaded, 16)
            sp.dma_start(gates_in[:, 1:2], g_ffn.partition_broadcast(P)).then_inc(gate_in_loaded, 16)
            sp.wait_ge(wg_zero, 1)
            sp.dma_start(wg_pad[:, :, 0:E], w_gate).then_inc(wg_loaded, 16)

            def load_expert(e, slot, done):
                sp.dma_start(ring[:, slot, :], experts[e]).then_inc(done, 16)
                sp.dma_start(bring[:, slot, :], expert_bias[e].partition_broadcast(P)).then_inc(done, 16)

            sp.wait_ge(exps_done, 1)
            sp.wait_ge(xs_zero, 1)
            for r in range(0, BLOCKS, ZROWS):
                n = min(ZROWS, BLOCKS - r)
                sp.dma_start(sorted_x[r * P:(r + n) * P, :].rearrange("(p t) n -> p t n", p=P),
                             ring[:, 2, 0:n * D].rearrange("p (t n) -> p t n", n=D)).then_inc(zeroed, 16)
            sp.dma_start(shared[:, :], shared_w).then_inc(shared_loaded, 16)
            sp.dma_start(bs2_bc[:, :], bs2.partition_broadcast(P)).then_inc(w_odd, 16)
            load_expert(0, 0, w_even)
            load_expert(1, 1, w_odd)
            sp.wait_ge(zeroed, 16 * ZDMAS)
            sp.wait_ge(w_even, 32)
            load_expert(2, 2, w_even)
            sp.wait_ge(table_ready, 1)

            def later(e, slot, done, before):
                sp.wait_ge(done, before)
                end = sp.value_load(blk_end[0:1, bass.ds(e - WSLOTS, 1)], min_val=1, max_val=BLOCKS)
                sp.wait_ge(y_ready, end)
                load_expert(e, slot, done)
            for e in range(WSLOTS, E):
                later(e, e % WSLOTS, w_odd if e % 2 else w_even, 32 * (e // 2) + 16 * (e % 2))

        @block.tensor
        def _(pe):
            mm, tr = nc.tensor.matmul, nc.tensor.transpose

            def project_xnT(j):
                pe.wait_ge(xn_ready, 2 * j + 2)
                for b in range(2):
                    for c in range(DC):
                        i = tr(work[:, (2 * c + b) * P:(2 * c + b + 1) * P], xn[:, b, c * P:(c + 1) * P], ident)
                i.then_inc(xnT_ps, 1)

            def project(w, src, done):
                for m in range(DC):
                    for c in range(DC):
                        i = mm(work[:, m * 2 * P:(m + 1) * 2 * P], wqkvo[:, w, c, m * P:(m + 1) * P], src[:, c, :],
                               start=(c == 0), stop=(c == DC - 1))
                i.then_inc(done, 1)

            def project_k(j):
                pe.wait_ge(ctx_loaded, 16 * j + 16)
                project(1, ctxT, k_ps)

            def project_q(j):
                pe.wait_ge(xnT_ready, j + 1)
                project(0, xnT, q_ps)

            def project_v(j):
                for b in range(2):
                    for c in range(DC):
                        i = mm(work[:, b * D:(b + 1) * D], ctxT[:, c, b * CTX:(b + 1) * CTX], wqkvo[:, 2, c, :],
                               start=(c == 0), stop=(c == DC - 1))
                i.then_inc(v_ps, 1)

            def scores(j, u):
                b, m = divmod(u, 2)
                n = 4 * j + u
                pe.wait_ge(kblk_ready, n + 1)
                if u == 0:
                    pe.wait_ge(qT_ready, j + 1)
                if not (isinstance(n, int) and n < 2):
                    pe.wait_ge(exps_done, n - 1)
                for hb in range(2):
                    i = mm(big[:, u % 2, hb, :], qT[:, m, b * P:(b + 1) * P],
                           kblk[:, u % 2, 4 * hb:4 * hb + 4, :].rearrange("p h k -> p (h k)"), start=True, stop=True)
                i.then_inc(scores_ready, 1)

            def transpose_probs(j, u):
                n = 4 * j + u
                pe.wait_ge(probs_ready, n + 1)
                for g in range(2):
                    if not (isinstance(n, int) and n < 1):
                        pe.wait_ge(pt_copied, 2 * n - 1 + g)
                    for h in range(4):
                        i = tr(mid[:, g, h * P:(h + 1) * P], probs[:, u % 2, 4 * g + h, :], ident)
                    i.then_inc(pt_ready, 1)

            def weigh_values(j, u):
                n = 4 * j + u
                pe.wait_ge(v_ready, j + 1)
                if not (isinstance(n, int) and n < 1):
                    pe.wait_ge(heads_copied, n)
                for h in range(HG):
                    if h % 4 == 0:
                        pe.wait_ge(pt_copied, 2 * n + h // 4 + 1)
                    i = mm(last[:, 0:P], vmask[:, u, h * P:(h + 1) * P], pT[:, h // 4, h % 4, :],
                           start=(h == 0), stop=(h == HG - 1))
                i.then_inc(av_ready, 1)

            def project_out(j, b):
                pe.wait_ge(heads_copied, 4 * j + 2 * b + 2)
                for m in range(DC):
                    i = mm(work[:, 0:D], outT[:, 2 * b + m, :], wqkvo[:, 3, m, :], start=(m == 0), stop=(m == DC - 1))
                i.then_inc(o_ps, 1)

            def transpose_xf(j):
                pe.wait_ge(xf_ready, 2 * j + 2)
                for b in range(2):
                    for c in range(DC):
                        i = tr(work[:, (2 * c + b) * P:(2 * c + b + 1) * P], xfs[:, b, c * P:(c + 1) * P], ident)
                i.then_inc(xfT_ps, 1)

            def router(j):
                pe.wait_ge(xfT_ready, j + 1)
                for b in range(2):
                    for c in range(DC):
                        i = mm(work[:, b * P:(b + 1) * P], xfT[:, c, b * P:(b + 1) * P], wg_pad[:, c, :],
                               start=(c == 0), stop=(c == DC - 1))
                i.then_inc(lg_ps, 1)

            def pair(j, ahead, behind):
                for u in range(UNITS):
                    if u < UNITS - 1:
                        scores(j, u + 1)
                    elif ahead:
                        scores(j + 1, 0)
                    if behind:
                        if u == 0:
                            pe.wait_ge(v_ready, j + 1)
                            project_out(j - 1, 0)
                        if u == 1:
                            pe.wait_ge(xnT_ready, j + 2) if ahead else pe.wait_ge(o_taken, 2 * j - 1)
                            project_out(j - 1, 1)
                        if u == 2:
                            pe.wait_ge(kT_ready, j + 2) if ahead else pe.wait_ge(o_taken, 2 * j)
                            transpose_xf(j - 1)
                        if u == 3:
                            if ahead:
                                pe.wait_ge(qT_ready, j + 2)
                            router(j - 1)
                    transpose_probs(j, u)
                    if ahead:
                        if u == 0:
                            pe.wait_ge(o_taken, 2 * j - 1) if behind else pe.wait_ge(v_ready, j + 1)
                            project_xnT(j + 1)
                        if u == 1:
                            pe.wait_ge(o_taken, 2 * j) if behind else pe.wait_ge(xnT_ready, j + 2)
                            project_k(j + 1)
                        if u == 2:
                            pe.wait_ge(xfT_ready, j) if behind else pe.wait_ge(kT_ready, j + 2)
                            project_q(j + 1)
                        if u == 3:
                            pe.wait_ge(lg_taken, j) if behind else pe.wait_ge(qT_ready, j + 2)
                            project_v(j + 1)
                    weigh_values(j, u)

            pe.wait_ge(const_loaded, 16)
            project_xnT(0)
            pe.wait_ge(attn_w_loaded, 16)
            pe.wait_ge(xnT_ready, 1)
            project_k(0)
            pe.wait_ge(kT_ready, 1)
            project_q(0)
            pe.wait_ge(qT_ready, 1)
            project_v(0)
            scores(0, 0)
            pe.wait_ge(wg_loaded, 16)
            pair(0, True, False)
            with pe.Fori(1, LAST) as j:
                pair(j, True, True)
            pair(LAST, False, True)
            pe.wait_ge(lg_taken, LAST)
            project_out(LAST, 0)
            pe.wait_ge(o_taken, 2 * LAST + 1)
            project_out(LAST, 1)
            pe.wait_ge(o_taken, 2 * LAST + 2)
            transpose_xf(LAST)
            router(LAST)

            pe.wait_ge(onehots_ready, 1)
            mm(mid[:, 0, 0:TILES * E], const[:, C_TRI:C_TRI + P], rt[:, 0, :], start=True, stop=True)
            mm(mid[:, 1, 0:TILES * E], const[:, C_ONE:C_ONE + P], rt[:, 0, :], start=True, stop=True).then_inc(rank_ps, 1)

            def shared_group(g, first):
                for c in range(SC):
                    n = SC * g + c
                    if not (first and c < 2):
                        pe.wait_ge(gsh_ready, n - 1)
                    for w, wt in enumerate((ws1, ws11)):
                        for k in range(DC):
                            i = mm(big[:, c % 2, w, :], wt[:, k, c * P:(c + 1) * P],
                                   xfT_all[:, k, bass.ds(512 * g, 512)], start=(k == 0), stop=(k == DC - 1))
                    i.then_inc(sh_ps, 1)
                pe.wait_ge(gsh_ready, SC * g + SC)
                for t in range(GROUP):
                    n = GROUP * g + t
                    if not (first and t < 2):
                        pe.wait_ge(z_taken, n - 1)
                    for c in range(SC):
                        i = mm(zbank[t % 2][:, 0:D], gshT[:, c, t * P:(t + 1) * P], ws2[:, c, :], start=(c == 0), stop=(c == SC - 1))
                    i.then_inc(z_ps, 1)

            pe.wait_ge(shared_loaded, 16)
            pe.wait_ge(xfT_kept, PAIRS)
            shared_group(0, True)
            shared_group(1, False)

            def expert_of(b):
                return pe.value_load(blk_expert[0:1, bass.ds(b, 1)], min_val=0, max_val=E - 1)

            def transpose_rows(b, p):
                pe.wait_ge(xs_odd if p else xs_even, 16 * ((b - p) // 2) + 16 if isinstance(b, int) else 8 * (b - p) + 16)
                if not (isinstance(b, int) and b < 1):
                    pe.wait_ge(xsT_ready, b)
                for c in range(DC):
                    i = tr(work[:, c * P:(c + 1) * P], xs[:, p, c * P:(c + 1) * P], ident)
                i.then_inc(xs_ps, 1)

            def up(b, p):
                e = expert_of(b)
                slot = pe.snap(e % WSLOTS)
                pe.wait_ge(w_even, pe.snap(32 * (e // 2) + 32))
                pe.wait_ge(w_odd, pe.snap(32 * ((e + 1) // 2) + 16))
                pe.wait_ge(xsT_ready, b + 1)
                if not (isinstance(b, int) and b < 2):
                    pe.wait_ge(h_taken, b - 1)
                for w in range(2):
                    for k in range(DC):
                        i = mm(big[:, p, w, :], xsT[:, p, k, :],
                               ring[:, slot, (w * DC + k) * HID:(w * DC + k + 1) * HID], start=(k == 0), stop=(k == DC - 1))
                i.then_inc(up_ps, 1)

            def transpose_hidden(b, p):
                pe.wait_ge(g_ready, b + 1)
                if not (isinstance(b, int) and b < 1):
                    pe.wait_ge(gT_ready, b)
                for c in range(HC):
                    i = tr(mid[:, 0, c * P:(c + 1) * P], gg[:, p, c * P:(c + 1) * P], ident)
                i.then_inc(gt_ps, 1)

            def down(b, p):
                slot = pe.snap(expert_of(b) % WSLOTS)
                pe.wait_ge(gT_ready, b + 1)
                if not (isinstance(b, int) and b < 1):
                    pe.wait_ge(y_ready, b)
                for c in range(HC):
                    o = 2 * DC * HID + c * D
                    i = mm(mid[:, 1, 0:D], gT[:, p, c, :], ring[:, slot, o:o + D], start=(c == 0), stop=(c == HC - 1))
                i.then_inc(down_ps, 1)

            pe.wait_ge(table_ready, 1)
            pe.wait_ge(rank_taken, 1)

            def slot(n, p, rows, ahead):
                if ahead:
                    up(n + 1, 1 - p)
                if rows:
                    transpose_rows(n + 3, 1 - p)
                transpose_hidden(n, p)
                down(n - 1, 1 - p)

            pe.wait_ge(z_taken, 2 * GROUP)
            transpose_rows(0, 0)
            transpose_rows(1, 1)
            up(0, 0)
            transpose_rows(2, 0)
            up(1, 1)
            transpose_rows(3, 1)
            transpose_hidden(0, 0)
            slot(1, 1, True, True)
            slot(2, 0, True, True)
            with pe.Fori(1, LOOPED // 2) as i:
                slot(2 * i + 1, 1, True, True)
                slot(2 * i + 2, 0, True, True)
            for n in range(LOOPED + 1, BLOCKS):
                slot(n, n % 2, n + 3 < BLOCKS, n + 1 < BLOCKS)
            down(BLOCKS - 1, (BLOCKS - 1) % 2)

            pe.wait_ge(h_taken, BLOCKS)
            shared_group(2, False)
            shared_group(3, False)

        @block.scalar
        def _(act):
            act.wait_ge(gate_in_loaded, 32)
            nc.scalar.activation(tanh_g[:, :], gates_in[:, :], ACT.Tanh).then_inc(tanh_ready, 1)

            def exps(j, u):
                n = 4 * j + u
                act.wait_ge(negmax_ready, n + 1)
                if not (isinstance(n, int) and n < 2):
                    act.wait_ge(pt_ready, 2 * n - 2)
                for h in range(HG):
                    i = nc.scalar.activation(probs[:, u % 2, h, :], big[:, u % 2, h // 4, (h % 4) * CTX:(h % 4 + 1) * CTX],
                                             ACT.Exp, bias=nmax[:, u % 2, h:h + 1], accum_out=rsum[:, u % 2, h:h + 1])
                i.then_inc(exps_done, 1)

            def copy_probs(j, u):
                n = 4 * j + u
                if not (isinstance(n, int) and n < 1):
                    act.wait_ge(av_ready, n)
                for g in range(2):
                    act.wait_ge(pt_ready, 2 * n + g + 1)
                    nc.scalar.activation(pT[:, g, :, :].rearrange("p h q -> p (h q)"), mid[:, g, :], ACT.Copy) \
                        .then_inc(pt_copied, 1)

            def copy_heads(j, u):
                n = 4 * j + u
                act.wait_ge(av_ready, n + 1)
                nc.scalar.activation(outT[:, u, :], last[:, 0:P], ACT.Identity, bias=bias[:, B_V + u % 2:B_V + u % 2 + 1]) \
                    .then_inc(heads_copied, 1)

            def load_context(j):
                act.wait_ge(v_ps, j)
                act.dma_start(ctxT, ctx_t[j]).then_inc(ctx_loaded, 16)

            def pair(j, ahead, ahead2):
                for u in range(UNITS):
                    copy_probs(j, u)
                    if u < UNITS - 1:
                        exps(j, u + 1)
                    elif ahead:
                        exps(j + 1, 0)
                    copy_heads(j, u)
                    if u == UNITS - 1 and ahead2:
                        load_context(j + 2)

            act.wait_ge(bias_loaded, 16)
            exps(0, 0)
            load_context(1)
            pair(0, True, True)
            with act.Fori(1, LAST - 1) as j:
                pair(j, True, True)
            pair(LAST - 1, True, False)
            pair(LAST, False, False)

            act.wait_ge(gate_exp_in, 1)
            nc.scalar.activation(gtmp[:, 1, :], gtmp[:, 0, :], ACT.Exp).then_inc(gate_exp, 1)

            def shared_group(g, first):
                for c in range(SC):
                    n = SC * g + c
                    act.wait_ge(sh_ps, n + 1)
                    if not (first and c < 2):
                        act.wait_ge(gsh_ready, n - 1)
                    nc.scalar.activation(sil[:, c % 2, :], big[:, c % 2, 0, :], ACT.Silu, bias=bias[:, B_S1 + c:B_S1 + c + 1]) \
                        .then_inc(silu_ready, 1)

            shared_group(0, True)
            shared_group(1, False)

            def silu(b, p):
                act.wait_ge(h1_ready, b + 1)
                if not (isinstance(b, int) and b < 2):
                    act.wait_ge(g_ready, b - 1)
                nc.scalar.activation(sl[:, p, :], hb1[:, p, :], ACT.Silu).then_inc(s_ready, 1)

            def copy_hidden(b, p):
                act.wait_ge(gt_ps, b + 1)
                if not (isinstance(b, int) and b < 2):
                    act.wait_ge(down_ps, b - 1)
                nc.scalar.activation(gT[:, p, :, :].rearrange("p c n -> p (c n)"), mid[:, 0, :], ACT.Copy).then_inc(gT_ready, 1)

            def slot(n, p, ahead):
                if ahead:
                    silu(n + 1, 1 - p)
                copy_hidden(n, p)

            silu(0, 0)
            silu(1, 1)
            copy_hidden(0, 0)
            slot(1, 1, True)
            slot(2, 0, True)
            with act.Fori(1, LOOPED // 2) as i:
                slot(2 * i + 1, 1, True)
                slot(2 * i + 2, 0, True)
            for n in range(LOOPED + 1, BLOCKS):
                slot(n, n % 2, n + 1 < BLOCKS)
            shared_group(2, False)
            shared_group(3, False)
            for t in range(TILES):
                act.wait_ge(combined, t + 1)
                act.wait_ge(z_added, t + 1)
                act.dma_start(out[:, t, :], x_all[:, t, :]).then_inc(stored, 16)
            act.wait_ge(stored, 16 * TILES)

        @block.vector
        def _(dve):
            v = nc.vector
            links = [0, 0]
            base = [0]

            def link(ins):
                links[0] += 1
                ins.then_inc(dve_step, 1)
                dve.wait_ge(dve_step, base[0] + links[0])

            def carry():
                v.memset(carrier[:, :], 0.0)

            def norm_var(src, mv, ve, b, done):
                carry()
                link(v.bn_stats(stats[:, b, :], src))
                carry()
                link(v.bn_aggr(mv[:, b, :], stats[:, b, :]))
                v.tensor_scalar(ve[:, b:b + 1], mv[:, b, 1:2], EPS, None, ALU.add).then_inc(done, 1)

            def ln1_stats(j, b):
                norm_var(x_all[:, 2 * j + b, :], mv1, ve1, b, ln1_var)

            def ln1_apply(j, b):
                dve.wait_ge(ln1_rstd, 2 * j + b + 1)
                if not (isinstance(j, int) and j < 1):
                    dve.wait_ge(xnT_ps, j)
                v.tensor_scalar(xn[:, b, :], x_all[:, 2 * j + b, :], mv1[:, b, 0:1], rs1[:, b:b + 1],
                                ALU.subtract, ALU.mult).then_inc(xn_ready, 1)

            def add_attention(j, b):
                n = 2 * j + b
                dve.wait_ge(o_ps, n + 1)
                ins = v.tensor_tensor(att[:, :], work[:, 0:D], bo_bc, ALU.add)
                ins.then_inc(o_taken, 1)
                dve.wait_ge(o_taken, n + 1)
                link(v.scalar_tensor_tensor(out=x_all[:, n, :], in0=att[:, :], scalar=tanh_g[:, 0:1], in1=x_all[:, n, :],
                                            op0=ALU.mult, op1=ALU.add))
                norm_var(x_all[:, n, :], mv2, ve2, b, ln2_var)

            def ln2_apply(j, b):
                n = 2 * j + b
                dve.wait_ge(ln2_rstd, n + 1)
                if not (isinstance(j, int) and j < 1):
                    dve.wait_ge(xf_kept, 2 * j)
                v.tensor_scalar(xfs[:, b, :], x_all[:, n, :], mv2[:, b, 0:1], rs2[:, b:b + 1],
                                ALU.subtract, ALU.mult).then_inc(xf_ready, 1)

            def row_max(j, u):
                n = 4 * j + u
                dve.wait_ge(scores_ready, n + 1)
                link(v.reduce_max(rmax[:, u % 2, :], big[:, u % 2, :, :].rearrange("p a (h k) -> p (a h) k", k=CTX), AX.X))
                v.tensor_scalar(nmax[:, u % 2, :], rmax[:, u % 2, :], -1.0, None, ALU.mult).then_inc(negmax_ready, 1)

            def row_inv(j, u):
                n = 4 * j + u
                dve.wait_ge(exps_done, n + 1)
                if not (isinstance(n, int) and n < 2):
                    dve.wait_ge(probs_ready, n - 1)
                v.reciprocal(rinv[:, u % 2, :], rsum[:, u % 2, :]).then_inc(rinv_ready, 1)

            def copy_xnT(j):
                dve.wait_ge(xnT_ps, j + 1)
                if not (isinstance(j, int) and j < 1):
                    dve.wait_ge(q_ps, j)
                v.tensor_copy(xnT.rearrange("p c n -> p (c n)"), work[:, :]).then_inc(xnT_ready, 1)

            def copy_k(j):
                dve.wait_ge(k_ps, j + 1)
                if not (isinstance(j, int) and j < 1):
                    dve.wait_ge(kblk_ready, 4 * j)
                for m in range(DC):
                    i = v.tensor_scalar(kT[:, m, :], work[:, m * 2 * P:(m + 1) * 2 * P], bias[:, B_K + m:B_K + m + 1], None, ALU.add)
                i.then_inc(kT_ready, 1)

            def copy_q(j):
                dve.wait_ge(q_ps, j + 1)
                if not (isinstance(j, int) and j < 1):
                    dve.wait_ge(scores_ready, 4 * j)
                for m in range(DC):
                    i = v.tensor_scalar(qT[:, m, :], work[:, m * 2 * P:(m + 1) * 2 * P], bias[:, B_Q + m:B_Q + m + 1], SCALE,
                                        ALU.add, ALU.mult)
                i.then_inc(qT_ready, 1)

            def copy_v(j):
                dve.wait_ge(v_ps, j + 1)
                if not (isinstance(j, int) and j < 1):
                    dve.wait_ge(av_ready, 4 * j)
                for u in range(UNITS):
                    i = v.tensor_copy(vmask[:, u, :].rearrange("p (h c) -> p h c", h=HG)[:, :, 0:DH],
                                      work[:, u * P:(u + 1) * P].rearrange("p (h c) -> p h c", h=HG))
                i.then_inc(v_ready, 1)

            def copy_xfT(j):
                dve.wait_ge(xfT_ps, j + 1)
                if not (isinstance(j, int) and j < 1):
                    dve.wait_ge(lg_ps, j)
                    dve.wait_ge(xfT_kept, j)
                v.tensor_copy(xfT[:, :, :].rearrange("p c n -> p (c n)"), work[:, :]).then_inc(xfT_ready, 1)

            def choose(j):
                dve.wait_ge(lg_ps, j + 1)
                ins = v.tensor_copy(logits[:, :, :], work[:, 0:2 * P].rearrange("p (b e) -> p b e", b=2)[:, :, 0:E])
                ins.then_inc(lg_taken, 1)
                dve.wait_ge(lg_taken, j + 1)
                carry()
                for b in range(2):
                    ins = v.max(top8[:, b, :], logits[:, b, :])
                link(ins)
                carry()
                for b in range(2):
                    ins = v.max_index(idx8[:, b, :], top8[:, b, :], logits[:, b, :])
                link(ins)
                link(v.tensor_copy(idxf[:, :, :], idx8[:, :, 0:TOPK]))
                for b in range(2):
                    for k in range(TOPK):
                        v.tensor_scalar(chosen[:, k, 2 * j + b, :], const[:, C_IE:C_IE + E], idxf[:, b, k:k + 1], None, ALU.is_equal)
                        ins = v.tensor_copy(top2[:, k, bass.ds(2 * j + b, 1)], top8[:, b, k:k + 1])
                link(ins)

            def pair(j, ahead, behind, ahead2):
                for u in range(UNITS):
                    if behind and u < 2:
                        add_attention(j - 1, u)
                    if behind and u == 2:
                        copy_xfT(j - 1)
                    if behind and u == 3:
                        choose(j - 1)
                    if ahead2 and u >= 2:
                        ln1_stats(j + 2, u - 2)
                    if u < UNITS - 1:
                        row_max(j, u + 1)
                    elif ahead:
                        row_max(j + 1, 0)
                    if behind and u < 2:
                        ln2_apply(j - 1, u)
                    if ahead2 and u >= 2:
                        ln1_apply(j + 2, u - 2)
                    if ahead:
                        (copy_xnT, copy_k, copy_q, copy_v)[u](j + 1)
                    if u < UNITS - 1:
                        row_inv(j, u + 1)
                    elif ahead:
                        row_inv(j + 1, 0)

            v.memset(mhalf[:, :], -0.5).then_inc(half_ready, 1)
            v.memset(wg_pad[:, :, :], 0.0).then_inc(wg_zero, 1)
            dve.wait_ge(x_head_loaded, 16)
            for b in range(2):
                ln1_stats(0, b)
            for b in range(2):
                ln1_apply(0, b)
            for b in range(2):
                ln1_stats(1, b)
            dve.wait_ge(const_loaded, 16)
            copy_xnT(0)
            for b in range(2):
                ln1_apply(1, b)
            dve.wait_ge(bias_loaded, 16)
            copy_k(0)
            copy_q(0)
            dve.wait_ge(vmask_zero, 1)
            copy_v(0)
            row_max(0, 0)
            row_inv(0, 0)
            dve.wait_ge(x_loaded, 16)
            dve.wait_ge(bo_loaded, 16)
            dve.wait_ge(tanh_ready, 1)
            pair(0, True, False, True)
            pair(1, True, True, True)
            before = links[0]
            LINKS = UNITS + 2 * 3 + 2 * 2 + 4
            with dve.Fori(2, LAST - 1) as j:
                base[0] = (j - 2) * LINKS
                pair(j, True, True, True)
            assert links[0] - before == LINKS, links[0] - before
            base[0] = (LAST - 4) * LINKS
            pair(LAST - 1, True, True, False)
            pair(LAST, False, True, False)
            for b in range(2):
                add_attention(LAST, b)
                ln2_apply(LAST, b)
            copy_xfT(LAST)
            choose(LAST)

            def r3(i):
                return rt[:, i, :].rearrange("p (t e) -> p t e", t=TILES)

            ins = v.tensor_tensor(r3(0), chosen[:, 0, :, :], chosen[:, 1, :, :], ALU.add)
            ins.then_inc(onehots_ready, 1)
            v.tensor_tensor(gtmp[:, 0, :], top2[:, 1, :], top2[:, 0, :], ALU.subtract).then_inc(gate_exp_in, 1)
            dve.wait_ge(rank_ps, 1)
            link(v.tensor_copy(rt[:, 1, :], mid[:, 1, 0:TILES * E]))
            cur, nxt, step = 1, 2, 1
            while step < TILES:
                v.tensor_copy(r3(nxt)[:, 0:step, :], r3(cur)[:, 0:step, :])
                link(v.tensor_tensor(r3(nxt)[:, step:, :], r3(cur)[:, step:, :], r3(cur)[:, :TILES - step, :], ALU.add))
                cur, nxt = nxt, 3 if nxt == 2 else 2
                step *= 2
            total = r3(cur)[:, TILES - 1, :]
            other = 2 if cur == 3 else 3
            cmp16 = blk_cmp[:, 0:TILES, :]
            link(v.tensor_tensor(cmp16, total.unsqueeze(1).to_broadcast([P, TILES, E]),
                                 const[:, C_IT:C_IT + TILES].unsqueeze(2).to_broadcast([P, TILES, E]), ALU.is_gt))
            link(v.tensor_reduce(cnt[:, 5, :], cmp16.rearrange("p t e -> p e t"), AX.X, ALU.add))
            link(v.tensor_scalar(cnt[:, 0, :], cnt[:, 5, :], 1.0, None, ALU.max))
            c_cur, c_nxt, step = 0, 1, 1
            while step < E:
                v.tensor_copy(cnt[:, c_nxt, 0:step], cnt[:, c_cur, 0:step])
                link(v.tensor_tensor(cnt[:, c_nxt, step:], cnt[:, c_cur, step:], cnt[:, c_cur, :E - step], ALU.add))
                c_cur, c_nxt = c_nxt, c_nxt + 1
                step *= 2
            ends = cnt[:, c_cur, :]
            v.tensor_copy(blk_end[:, :], ends)
            link(v.tensor_tensor(blk_cmp[:, :, :], ends.unsqueeze(1).to_broadcast([P, BLOCKS, E]),
                                 const[:, C_IB:C_IB + BLOCKS].unsqueeze(2).to_broadcast([P, BLOCKS, E]), ALU.is_le))
            link(v.tensor_reduce(blk_f[:, :], blk_cmp[:, :, :], AX.X, ALU.add))
            v.tensor_scalar(blk_expert[:, :], blk_f[:, :], float(E - 1), None, ALU.min).then_inc(table_ready, 1)
            link(v.tensor_tensor(cnt[:, 5, :], ends, cnt[:, 0, :], ALU.subtract))
            link(v.tensor_tensor(r3(other), r3(cur), r3(1), ALU.subtract))
            link(v.scalar_tensor_tensor(out=r3(cur), in0=cnt[:, 5, :].unsqueeze(1).to_broadcast([P, TILES, E]), scalar=float(P),
                                        in1=r3(other), op0=ALU.mult, op1=ALU.add))
            ins = v.tensor_tensor(r3(other), r3(cur), mid[:, 0, 0:TILES * E].rearrange("p (t e) -> p t e", t=TILES), ALU.add)
            ins.then_inc(rank_taken, 1)
            dve.wait_ge(rank_taken, 1)
            for k in range(TOPK):
                link(v.tensor_tensor(r3(0), chosen[:, k, :, :], r3(other), ALU.mult))
                link(v.tensor_reduce(pos_f[:, k, :], r3(0), AX.X, ALU.add))
            v.tensor_copy(pos[:, :, :], pos_f[:, :, :]).then_inc(pos_ready, 1)
            dve.wait_ge(gate_exp, 1)
            link(v.tensor_scalar(gtmp[:, 2, :], gtmp[:, 1, :], 1.0, None, ALU.add))
            link(v.reciprocal(gtmp[:, 0, :], gtmp[:, 2, :]))
            link(v.tensor_scalar(gate[:, 0, :], gtmp[:, 0, :], tanh_g[:, 1:2], None, ALU.mult))
            v.tensor_tensor(gate[:, 1, :], gate[:, 0, :], gtmp[:, 1, :], ALU.mult).then_inc(gates_ready, 1)

            def shared_hidden(g):
                for c in range(SC):
                    n = SC * g + c
                    dve.wait_ge(silu_ready, n + 1)
                    if g > 0:
                        dve.wait_ge(z_ps, GROUP * g)
                    v.scalar_tensor_tensor(out=gshT[:, c, :], in0=big[:, c % 2, 1, :], scalar=bias[:, B_S11 + c:B_S11 + c + 1],
                                           in1=sil[:, c % 2, :], op0=ALU.add, op1=ALU.mult).then_inc(gsh_ready, 1)
            def add_shared(g):
                for t in range(GROUP):
                    n = GROUP * g + t
                    dve.wait_ge(z_ps, n + 1)
                    v.tensor_tensor(zt, zbank[t % 2][:, 0:D], bs2_bc[:, :], ALU.add).then_inc(z_taken, 1)
                    dve.wait_ge(z_taken, n + 1)
                    v.scalar_tensor_tensor(out=x_all[:, n, :], in0=zt, scalar=tanh_g[:, 1:2], in1=x_all[:, n, :],
                                           op0=ALU.mult, op1=ALU.add).then_inc(z_added, 1)
                    dve.wait_ge(z_added, n + 1)

            dve.wait_ge(w_odd, 16 + 32)
            for g in range(2):
                shared_hidden(g)
                add_shared(g)

            def copy_rows(b, p):
                dve.wait_ge(xs_ps, b + 1)
                if not (isinstance(b, int) and b < 2):
                    dve.wait_ge(up_ps, b - 1)
                v.tensor_copy(xsT[:, p, :, :].rearrange("p c n -> p (c n)"), work[:, 0:D]).then_inc(xsT_ready, 1)

            def slot_of(b):
                e = dve.value_load(blk_expert[0:1, bass.ds(b, 1)], min_val=0, max_val=E - 1)
                return dve.snap(e % WSLOTS)

            def add_biases(b, p):
                slot = slot_of(b)
                dve.wait_ge(up_ps, b + 1)
                if not (isinstance(b, int) and b < 2):
                    dve.wait_ge(s_ready, b - 1)
                    dve.wait_ge(g_ready, b - 1)
                v.tensor_tensor(hb1[:, p, :], big[:, p, 0, :], bring[:, slot, 0:HID], ALU.add).then_inc(h1_ready, 1)
                v.tensor_tensor(hb11[:, p, :], big[:, p, 1, :], bring[:, slot, HID:2 * HID], ALU.add).then_inc(h_taken, 1)

            def hidden(b, p):
                dve.wait_ge(s_ready, b + 1)
                dve.wait_ge(h_taken, b + 1)
                if not (isinstance(b, int) and b < 2):
                    dve.wait_ge(gt_ps, b - 1)
                v.tensor_tensor(gg[:, p, :], sl[:, p, :], hb11[:, p, :], ALU.mult).then_inc(g_ready, 1)

            def add_out_bias(b, p):
                slot = slot_of(b)
                dve.wait_ge(down_ps, b + 1)
                if not (isinstance(b, int) and b < 2):
                    dve.wait_ge(y_st_odd if p else y_st_even, 8 * (b - p))
                v.tensor_tensor(ysb[:, p, :], mid[:, 1, 0:D], bring[:, slot, 2 * HID:BCOLS], ALU.add).then_inc(y_ready, 1)

            dve.wait_ge(table_ready, 1)
            def slot(n, p, rows, ahead):
                if ahead:
                    add_biases(n + 1, 1 - p)
                if rows:
                    copy_rows(n + 3, 1 - p)
                if ahead:
                    hidden(n + 1, 1 - p)
                add_out_bias(n - 1, 1 - p)

            copy_rows(0, 0)
            copy_rows(1, 1)
            add_biases(0, 0)
            copy_rows(2, 0)
            hidden(0, 0)
            add_biases(1, 1)
            copy_rows(3, 1)
            hidden(1, 1)
            slot(1, 1, True, True)
            slot(2, 0, True, True)
            with dve.Fori(1, LOOPED // 2) as i:
                slot(2 * i + 1, 1, True, True)
                slot(2 * i + 2, 0, True, True)
            for n in range(LOOPED + 1, BLOCKS):
                slot(n, n % 2, n + 3 < BLOCKS, n + 1 < BLOCKS)
            add_out_bias(BLOCKS - 1, (BLOCKS - 1) % 2)

            def combine(t):
                n = t % GATHERS
                dve.wait_ge(gathered_b if t >= GATHERS else gathered, 32 * GATHERS)
                link(v.scalar_tensor_tensor(out=x_all[:, t, :], in0=yg[:, n, 0, :], scalar=gate[:, 0, t:t + 1], in1=x_all[:, t, :],
                                            op0=ALU.mult, op1=ALU.add))
                v.scalar_tensor_tensor(out=x_all[:, t, :], in0=yg[:, n, 1, :], scalar=gate[:, 1, t:t + 1], in1=x_all[:, t, :],
                                       op0=ALU.mult, op1=ALU.add).then_inc(combined, 1)

            dve.wait_ge(gates_ready, 1)
            shared_hidden(2)
            add_shared(2)
            for t in range(GATHERS):
                combine(t)
            shared_hidden(3)
            for t in range(GATHERS, TILES):
                combine(t)
            add_shared(3)

        @block.gpsimd
        def _(pool):
            g = nc.gpsimd

            def rstd1(j, b):
                pool.wait_ge(ln1_var, 2 * j + b + 1)
                if not (isinstance(j, int) and j < 1):
                    pool.wait_ge(xn_ready, 2 * j)
                g.tensor_tensor(rs1[:, b:b + 1], ve1[:, b:b + 1], mhalf[:, :], ALU.pow).then_inc(ln1_rstd, 1)

            def rstd2(j, b):
                pool.wait_ge(ln2_var, 2 * j + b + 1)
                if not (isinstance(j, int) and j < 1):
                    pool.wait_ge(xf_ready, 2 * j)
                g.tensor_tensor(rs2[:, b:b + 1], ve2[:, b:b + 1], mhalf[:, :], ALU.pow).then_inc(ln2_rstd, 1)

            def spread_keys(j, u):
                b, m = divmod(u, 2)
                n = 4 * j + u
                if u == 0:
                    pool.wait_ge(kT_ready, j + 1)
                if not (isinstance(n, int) and n < 2):
                    pool.wait_ge(scores_ready, n - 1)
                g.tensor_tensor(kblk[:, u % 2, :, :],
                                kT[:, m, b * CTX:(b + 1) * CTX].unsqueeze(1).to_broadcast([P, HG, CTX]),
                                const[:, C_HM:C_HM + HG].unsqueeze(2).to_broadcast([P, HG, CTX]), ALU.mult) \
                    .then_inc(kblk_ready, 1)

            def normalise(j, u):
                n = 4 * j + u
                pool.wait_ge(rinv_ready, n + 1)
                g.tensor_tensor(probs[:, u % 2, :, :], probs[:, u % 2, :, :],
                                rinv[:, u % 2, :].unsqueeze(2).to_broadcast([P, HG, CTX]), ALU.mult).then_inc(probs_ready, 1)

            def keep_xf(j, b):
                pool.wait_ge(xf_ready, 2 * j + b + 1)
                g.tensor_copy(xf_all[:, 2 * j + b, :], xfs[:, b, :]).then_inc(xf_kept, 1)

            def keep_xfT(j):
                pool.wait_ge(xfT_ready, j + 1)
                g.tensor_copy(xfT_all[:, :, bass.ds(2 * P * j, 2 * P)], xfT[:, :, :]).then_inc(xfT_kept, 1)

            def pair(j, ahead, behind, ahead2):
                for u in range(UNITS):
                    if behind and u < 2:
                        rstd2(j - 1, u)
                    if ahead2 and u >= 2:
                        rstd1(j + 2, u - 2)
                    if u < 2:
                        spread_keys(j, u + 2)
                    elif ahead:
                        spread_keys(j + 1, u - 2)
                    if u < UNITS - 1:
                        normalise(j, u + 1)
                    elif ahead:
                        normalise(j + 1, 0)
                    if behind and u in (1, 2):
                        keep_xf(j - 1, u - 1)
                    if behind and u == 3:
                        keep_xfT(j - 1)

            pool.wait_ge(half_ready, 1)
            for b in range(2):
                rstd1(0, b)
            for b in range(2):
                rstd1(1, b)
            g.memset(vmask, 0.0).then_inc(vmask_zero, 1)
            g.memset(ring[:, 2, :], 0.0).then_inc(xs_zero, 1)
            pool.wait_ge(const_loaded, 16)
            spread_keys(0, 0)
            spread_keys(0, 1)
            normalise(0, 0)
            pair(0, True, False, True)
            pair(1, True, True, True)
            with pool.Fori(2, LAST - 1) as j:
                pair(j, True, True, True)
            pair(LAST - 1, True, True, False)
            pair(LAST, False, True, False)
            for b in range(2):
                rstd2(LAST, b)
            for b in range(2):
                keep_xf(LAST, b)
            keep_xfT(LAST)

            pool.wait_ge(pos_ready, 1)
            pool.wait_ge(xf_kept, TILES)
            pool.wait_ge(zeroed, 16 * ZDMAS)
            for t in range(TILES):
                for k in range(TOPK):
                    g.indirect_dma_start(out=sorted_x, out_offset=bass.IndirectOffsetOnAxis(ap=pos[:, k, t:t + 1], axis=0),
                                         in_=xf_all[:, t, :], in_offset=None).then_inc(scattered, 16)
            pool.wait_ge(scattered, 16 * TILES * TOPK)

            def load_rows(b, p):
                if not (isinstance(b, int) and b < 2):
                    pool.wait_ge(xs_ps, b - 1)
                pool.dma_start(xs[:, p, :], sorted_x[bass.ds(b * P, P), :]).then_inc(xs_odd if p else xs_even, 16)

            def store_rows(b, p):
                pool.wait_ge(y_ready, b + 1)
                pool.dma_start(sorted_y[bass.ds(b * P, P), :], ysb[:, p, :]).then_inc(y_st_odd if p else y_st_even, 16)

            def slot(n, p, rows):
                if rows:
                    load_rows(n + 4, p)
                store_rows(n - 1, 1 - p)

            for b in range(5):
                load_rows(b, b % 2)
            slot(1, 1, True)
            slot(2, 0, True)
            with pool.Fori(1, LOOPED // 2) as i:
                slot(2 * i + 1, 1, True)
                slot(2 * i + 2, 0, True)
            for n in range(LOOPED + 1, BLOCKS):
                slot(n, n % 2, n + 4 < BLOCKS)
            store_rows(BLOCKS - 1, (BLOCKS - 1) % 2)
            pool.wait_ge(y_st_even, 16 * ((BLOCKS + 1) // 2))
            pool.wait_ge(y_st_odd, 16 * (BLOCKS // 2))
            for t in range(TILES):
                if t >= GATHERS:
                    pool.wait_ge(combined, t - GATHERS + 1)
                for k in range(TOPK):
                    g.indirect_dma_start(out=yg[:, t % GATHERS, k, :], out_offset=None, in_=sorted_y,
                                         in_offset=bass.IndirectOffsetOnAxis(ap=pos[:, k, t:t + 1], axis=0)) \
                        .then_inc(gathered_b if t >= GATHERS else gathered, 16)


def kernel(x, ctx_1024, g_xattn, g_ffn, L0_xattn_Wq, L0_xattn_bq, L0_xattn_Wk, L0_xattn_bk, L0_xattn_Wv, L0_xattn_bv,
           L0_xattn_Wo, L0_xattn_bo, L0_ffn_Wg, L0_ffn_W1, L0_ffn_b1, L0_ffn_W11, L0_ffn_b11, L0_ffn_W2, L0_ffn_b2,
           L0_ffn_Ws1, L0_ffn_bs1, L0_ffn_Ws11, L0_ffn_bs11, L0_ffn_Ws2, L0_ffn_bs2):
    import numpy as np
    import concourse.bacc as bacc
    from concourse.bass_utils import run_bass_kernel_spmd

    def rows(w):
        w = np.asarray(w)
        return w.reshape(w.shape[0] // P, P, w.shape[1]).transpose(1, 0, 2)

    def cols(v):
        return np.asarray(v).reshape(-1, P).T

    attn_w = np.stack([rows(np.asarray(w).T) for w in (L0_xattn_Wq, L0_xattn_Wk, L0_xattn_Wv, L0_xattn_Wo)], axis=1)
    col_bias = np.concatenate([cols(v) for v in (L0_xattn_bq, L0_xattn_bk, L0_xattn_bv, L0_ffn_bs1, L0_ffn_bs11)], axis=1)

    def expert_rows(w):
        w = np.asarray(w)
        return w.reshape(E, w.shape[1] // P, P, w.shape[2]).transpose(0, 2, 1, 3).reshape(E, P, -1)

    experts = np.concatenate([expert_rows(w) for w in (L0_ffn_W1, L0_ffn_W11, L0_ffn_W2)], axis=2)
    expert_bias = np.concatenate([np.asarray(b) for b in (L0_ffn_b1, L0_ffn_b11, L0_ffn_b2)], axis=1)
    shared_w = np.concatenate([rows(w).reshape(P, -1) for w in (L0_ffn_Ws1, L0_ffn_Ws11, L0_ffn_Ws2)], axis=1)

    i = np.arange(P)
    consts = np.zeros((P, CONSTS), np.float32)
    consts[:, C_ID:C_ID + P] = np.eye(P)
    consts[:, C_TRI:C_TRI + P] = i[:, None] < i[None, :]
    consts[:, C_ONE:C_ONE + P] = 1
    consts[:, C_HM:C_HM + HG] = i[:, None] // DH == np.arange(HG)[None, :]
    consts[:, C_IE:C_IE + E] = np.arange(E)
    consts[:, C_IB:C_IB + BLOCKS] = np.arange(BLOCKS)
    consts[:, C_IT:C_IT + TILES] = np.arange(TILES) * P

    ins = {
        "x": np.asarray(x).transpose(1, 0, 2),
        "ctx_t": np.asarray(ctx_1024).reshape(PAIRS, 2 * CTX, DC, P).transpose(0, 3, 2, 1),
        "attn_w": attn_w, "col_bias": col_bias, "bo": np.asarray(L0_xattn_bo),
        "g_xattn": np.asarray(g_xattn), "g_ffn": np.asarray(g_ffn), "w_gate": rows(L0_ffn_Wg),
        "experts": experts, "expert_bias": expert_bias, "shared_w": shared_w, "bs2": np.asarray(L0_ffn_bs2),
        "consts": consts,
    }
    nc = bacc.Bacc("TRN2", target_bir_lowering=False, num_devices=1)
    arrays, args = {}, []
    for name, a in ins.items():
        arrays[f"{name}_dram"] = a = np.ascontiguousarray(a)
        args.append(nc.dram_tensor(f"{name}_dram", a.shape, mybir.dt.from_np(a.dtype), kind="ExternalInput").ap())
    args.append(nc.dram_tensor("out_dram", (P, TILES, D), F32, kind="ExternalOutput").ap())
    flamingo_layer(nc, *args)
    r = run_bass_kernel_spmd(nc, [arrays], core_ids=[0])
    return np.ascontiguousarray(r.results[0]["out_dram"].transpose(1, 0, 2))
```

```python
from contextlib import ExitStack

import concourse.bass as bass
from concourse import mybir

P = 128
F32 = mybir.dt.float32
I32 = mybir.dt.int32
U32 = mybir.dt.uint32
ALU = mybir.AluOpType
ACT = mybir.ActivationFunctionType
AX = mybir.AxisListType

TILES = 16
D = 256
DC = D // P
CTX = 128
NH = 16
DH = D // NH
HG = P // DH
E = 16
HID = 512
HC = HID // P
SHID = 1024
SC = SHID // P
EPS = 1e-5
SCALE = DH ** -0.5
PAIRS = TILES // 2
UNITS = 4
TOKENS = TILES * P
TOPK = 2
BLOCKS = (TOPK * TOKENS + E * (P - 1)) // P
ROWS = BLOCKS * P
XBUFS = 4
AHEAD = 6
LOOPED = (BLOCKS - 1 - AHEAD) // 4 * 4
WSLOTS = 3
WCOLS = 2 * DC * HID + HC * D
BCOLS = 2 * HID + D
ZROWS = WCOLS // D
ZDMAS = -(-BLOCKS // ZROWS)
GROUP = 4
GATHERS = 8

C_ID, C_TRI, C_ONE, C_HM = 0, P, 2 * P, 3 * P
C_IE = C_HM + HG
C_IB = C_IE + E
C_IT = C_IB + BLOCKS
CONSTS = C_IT + TILES
B_Q, B_K, B_V, B_S1, B_S11 = 0, DC, 2 * DC, 3 * DC, 3 * DC + SC
BIASES = 3 * DC + 2 * SC


def flamingo_layer(nc, x, ctx_t, attn_w, col_bias, bo, g_xattn, g_ffn, w_gate, experts, expert_bias,
                   shared_w, bs2, consts, out):
    es = ExitStack()
    with es:
        def sb(name, shape, dt=F32):
            return es.enter_context(nc.sbuf_tensor(name, shape, dt))

        def sem(name):
            return es.enter_context(nc.semaphore(name))

        sorted_x = nc.dram_tensor("sorted_x", (ROWS, D), F32, kind="Internal").ap()
        sorted_y = nc.dram_tensor("sorted_y", (ROWS, D), F32, kind="Internal").ap()

        big = es.enter_context(nc.psum_tensor("big", [P, 2, 2, 512], F32))
        mid = es.enter_context(nc.psum_tensor("mid", [P, 2, 512], F32))
        work = es.enter_context(nc.psum_tensor("work", [P, 512], F32))
        last = es.enter_context(nc.psum_tensor("last", [P, 512], F32))

        zbank = (last, work)

        const = sb("const", [P, CONSTS])
        ident = const[:, C_ID:C_ID + P]
        bias = sb("bias", [P, BIASES])
        tanh_g = sb("tanh_g", [P, 2])
        gates_in = sb("gates_in", [P, 2])
        x_all = sb("x_all", [P, TILES, D])
        xf_all = sb("xf_all", [P, TILES, D])
        xfT_all = sb("xfT_all", [P, DC, TOKENS])
        bs2_bc = sb("bs2_bc", [P, D])
        shared = sb("shared", [P, 2 * DC * SHID + SC * D])
        ws1 = shared[:, 0:DC * SHID].rearrange("p (c n) -> p c n", c=DC)
        ws11 = shared[:, DC * SHID:2 * DC * SHID].rearrange("p (c n) -> p c n", c=DC)
        ws2 = shared[:, 2 * DC * SHID:].rearrange("p (c n) -> p c n", c=SC)
        ring = sb("ring", [P, WSLOTS, WCOLS])
        bring = sb("bring", [P, WSLOTS, BCOLS])

        logits = sb("logits", [P, 2, E])
        top8 = sb("top8", [P, 2, 8])
        idx8 = sb("idx8", [P, 2, 8], U32)
        idxf = sb("idxf", [P, 2, 2])
        chosen = sb("chosen", [P, TOPK, TILES, E])
        top2 = sb("top2", [P, TOPK, TILES])
        cnt = sb("cnt", [P, 6, E])
        pos_f = sb("pos_f", [P, TOPK, TILES])
        pos = sb("pos", [P, TOPK, TILES], U32)
        gate = sb("gate", [P, TOPK, TILES])
        gtmp = sb("gtmp", [P, 3, TILES])
        blk_f = sb("blk_f", [P, BLOCKS])
        blk_expert = sb("blk_expert", [P, BLOCKS], I32)
        blk_end = sb("blk_end", [P, E], I32)

        ARENA = 17920
        arena = sb("arena", [P, ARENA])
        taken = [0]

        def part(cols):
            taken[0] += cols
            assert taken[0] <= ARENA, taken[0]
            return arena[:, taken[0] - cols:taken[0]]

        kblk = part(2 * HG * CTX).rearrange("p (s h k) -> p s h k", s=2, h=HG)
        probs = part(2 * HG * CTX).rearrange("p (s h k) -> p s h k", s=2, h=HG)
        pT = part(2 * 4 * P).rearrange("p (g h q) -> p g h q", g=2, h=4)
        wqkvo = part(4 * DC * D).rearrange("p (w c n) -> p w c n", w=4, c=DC)
        VB = HG * (P + DH)
        vmask = part(4 * VB).rearrange("p (u c) -> p u c", u=UNITS)
        xn = part(2 * D).rearrange("p (b n) -> p b n", b=2)
        xnT = part(DC * 2 * P).rearrange("p (c n) -> p c n", c=DC)
        ctxT = part(DC * 2 * CTX).rearrange("p (c n) -> p c n", c=DC)
        qT = part(DC * 2 * P).rearrange("p (c n) -> p c n", c=DC)
        kT = part(DC * 2 * CTX).rearrange("p (c n) -> p c n", c=DC)
        outT = part(UNITS * P).rearrange("p (u q) -> p u q", u=UNITS)
        vflat = part(2 * D).rearrange("p (u c) -> p u c", u=UNITS)
        bo_bc = part(D)
        taken[0] = 0
        gshT = part(SC * 512).rearrange("p (c n) -> p c n", c=SC)
        sil = part(2 * 512).rearrange("p (s n) -> p s n", s=2)
        rt = part(4 * TILES * E).rearrange("p (i n) -> p i n", i=4)
        blk_cmp = part(BLOCKS * E).rearrange("p (b e) -> p b e", e=E)
        taken[0] -= (4 * TILES + BLOCKS) * E
        hb1 = part(2 * HID).rearrange("p (s n) -> p s n", s=2)
        hb11 = part(2 * HID).rearrange("p (s n) -> p s n", s=2)
        sl = part(2 * HID).rearrange("p (s n) -> p s n", s=2)
        gg = part(2 * HID).rearrange("p (s n) -> p s n", s=2)
        gT = part(2 * HID).rearrange("p (s c n) -> p s c n", s=2, c=HC)
        xs = part(XBUFS * D).rearrange("p (s n) -> p s n", s=XBUFS)
        xsT = part(2 * D).rearrange("p (s c n) -> p s c n", s=2, c=DC)
        ysb = part(2 * D).rearrange("p (s n) -> p s n", s=2)
        zt = part(D)
        yg = part(GATHERS * TOPK * D).rearrange("p (t k n) -> p t k n", t=GATHERS, k=TOPK)

        xfs = sb("xfs", [P, 2, D])
        xfT = sb("xfT", [P, DC, 2 * P])
        wg_pad = sb("wg_pad", [P, DC, P])
        stats = sb("stats", [P, 2, 6])
        mv1 = sb("mv1", [P, 2, 2])
        mv2 = sb("mv2", [P, 2, 2])
        ve1 = sb("ve1", [P, 2])
        ve2 = sb("ve2", [P, 2])
        rs1 = sb("rs1", [P, 2])
        rs2 = sb("rs2", [P, 2])
        mhalf = sb("mhalf", [P, 1])
        carrier = sb("carrier", [P, 1])
        rmax = sb("rmax", [P, 2, HG])
        nmax = sb("nmax", [P, 2, HG])
        rsum = sb("rsum", [P, 2, HG])
        rinv = sb("rinv", [P, 2, HG])
        att = sb("att", [P, D])

        gT_ready = sem("gT_ready")
        kT_ready = sem("kT_ready")
        qT_ready = sem("qT_ready")
        xfT_kept = sem("xfT_kept")
        xfT_ps = sem("xfT_ps")
        xfT_ready = sem("xfT_ready")
        xnT_ps = sem("xnT_ps")
        xnT_ready = sem("xnT_ready")
        xsT_ready = sem("xsT_ready")
        const_loaded = sem("const_loaded")
        bias_loaded = sem("bias_loaded")
        x_head_loaded = sem("x_head_loaded")
        x_loaded = sem("x_loaded")
        ctx_loaded = sem("ctx_loaded")
        attn_w_loaded = sem("attn_w_loaded")
        gate_in_loaded = sem("gate_in_loaded")
        wg_loaded = sem("wg_loaded")
        bo_loaded = sem("bo_loaded")
        shared_loaded = sem("shared_loaded")
        zeroed = sem("zeroed")
        tanh_ready = sem("tanh_ready")
        wg_zero = sem("wg_zero")
        half_ready = sem("half_ready")
        vmask_zero = sem("vmask_zero")
        xs_zero = sem("xs_zero")
        dve_step = sem("dve_step")
        ln1_var = sem("ln1_var")
        ln1_rstd = sem("ln1_rstd")
        ln2_var = sem("ln2_var")
        ln2_rstd = sem("ln2_rstd")
        xn_ready = sem("xn_ready")
        k_ps = sem("k_ps")
        q_ps = sem("q_ps")
        v_ps = sem("v_ps")
        v_copied = sem("v_copied")
        v_ready = sem("v_ready")
        kblk_ready = sem("kblk_ready")
        scores_ready = sem("scores_ready")
        negmax_ready = sem("negmax_ready")
        exps_done = sem("exps_done")
        rinv_ready = sem("rinv_ready")
        probs_ready = sem("probs_ready")
        pt_ready = sem("pt_ready")
        pt_copied = sem("pt_copied")
        av_ready = sem("av_ready")
        heads_copied = sem("heads_copied")
        o_ps = sem("o_ps")
        o_taken = sem("o_taken")
        xf_ready = sem("xf_ready")
        xf_kept = sem("xf_kept")
        lg_ps = sem("lg_ps")
        lg_taken = sem("lg_taken")
        onehots_ready = sem("onehots_ready")
        rank_ps = sem("rank_ps")
        rank_taken = sem("rank_taken")
        table_ready = sem("table_ready")
        pos_ready = sem("pos_ready")
        gate_exp_in = sem("gate_exp_in")
        gate_exp = sem("gate_exp")
        scattered = sem("scattered")
        w_even = sem("w_even")
        w_odd = sem("w_odd")
        xs0_loaded = sem("xs0_loaded")
        xs1_loaded = sem("xs1_loaded")
        xs2_loaded = sem("xs2_loaded")
        xs3_loaded = sem("xs3_loaded")
        xs_loaded = (xs0_loaded, xs1_loaded, xs2_loaded, xs3_loaded)
        xs_ps = sem("xs_ps")
        up_ps = sem("up_ps")
        h1_ready = sem("h1_ready")
        h_taken = sem("h_taken")
        s_ready = sem("s_ready")
        g_ready = sem("g_ready")
        gt_ps = sem("gt_ps")
        down_ps = sem("down_ps")
        y_ready = sem("y_ready")
        y_st_even = sem("y_st_even")
        y_st_odd = sem("y_st_odd")
        sh_ps = sem("sh_ps")
        silu_ready = sem("silu_ready")
        gsh_ready = sem("gsh_ready")
        z_ps = sem("z_ps")
        z_taken = sem("z_taken")
        z_added = sem("z_added")
        gathered = sem("gathered")
        gathered_b = sem("gathered_b")
        combined = sem("combined")
        gates_ready = sem("gates_ready")
        stored = sem("stored")

        block = es.enter_context(nc.Block())
        N_SH = 2 * SC
        LAST = PAIRS - 1

        @block.sync
        def _(sp):
            sp.dma_start(x_all[:, 0:4, :], x[:, 0:4, :]).then_inc(x_head_loaded, 16)
            sp.dma_start(const[:, :], consts).then_inc(const_loaded, 16)
            sp.dma_start(ctxT, ctx_t[0]).then_inc(ctx_loaded, 16)
            sp.dma_start(wqkvo, attn_w).then_inc(attn_w_loaded, 16)
            sp.dma_start(bias[:, :], col_bias).then_inc(bias_loaded, 16)
            sp.dma_start(x_all[:, 4:TILES, :], x[:, 4:TILES, :]).then_inc(x_loaded, 16)
            sp.dma_start(bo_bc, bo.partition_broadcast(P)).then_inc(bo_loaded, 16)
            sp.dma_start(gates_in[:, 0:1], g_xattn.partition_broadcast(P)).then_inc(gate_in_loaded, 16)
            sp.dma_start(gates_in[:, 1:2], g_ffn.partition_broadcast(P)).then_inc(gate_in_loaded, 16)
            sp.wait_ge(wg_zero, 1)
            sp.dma_start(wg_pad[:, :, 0:E], w_gate).then_inc(wg_loaded, 16)

            def load_expert(e, slot, done):
                sp.dma_start(ring[:, slot, :], experts[e]).then_inc(done, 16)
                sp.dma_start(bring[:, slot, :], expert_bias[e].partition_broadcast(P)).then_inc(done, 16)

            sp.wait_ge(exps_done, 1)
            sp.wait_ge(xs_zero, 1)
            for r in range(0, BLOCKS, ZROWS):
                n = min(ZROWS, BLOCKS - r)
                sp.dma_start(sorted_x[r * P:(r + n) * P, :].rearrange("(p t) n -> p t n", p=P),
                             ring[:, 2, 0:n * D].rearrange("p (t n) -> p t n", n=D)).then_inc(zeroed, 16)
            sp.wait_ge(ctx_loaded, 48)
            sp.dma_start(shared[:, :], shared_w).then_inc(shared_loaded, 16)
            sp.dma_start(bs2_bc[:, :], bs2.partition_broadcast(P)).then_inc(w_odd, 16)
            sp.wait_ge(ctx_loaded, 64)
            load_expert(0, 0, w_even)
            load_expert(1, 1, w_odd)
            sp.wait_ge(zeroed, 16 * ZDMAS)
            sp.wait_ge(w_even, 32)
            load_expert(2, 2, w_even)
            sp.wait_ge(table_ready, 1)

            def later(e, slot, done, before):
                sp.wait_ge(done, before)
                end = sp.value_load(blk_end[0:1, bass.ds(e - WSLOTS, 1)], min_val=1, max_val=BLOCKS)
                sp.wait_ge(y_ready, end)
                load_expert(e, slot, done)
            for e in range(WSLOTS, E):
                later(e, e % WSLOTS, w_odd if e % 2 else w_even, 32 * (e // 2) + 16 * (e % 2))

        @block.tensor
        def _(pe):
            mm, tr = nc.tensor.matmul, nc.tensor.transpose

            def project_xnT(j):
                pe.wait_ge(xn_ready, 2 * j + 2)
                for b in range(2):
                    for c in range(DC):
                        i = tr(work[:, (2 * c + b) * P:(2 * c + b + 1) * P], xn[:, b, c * P:(c + 1) * P], ident)
                i.then_inc(xnT_ps, 1)

            def project(w, src, done):
                for m in range(DC):
                    for c in range(DC):
                        i = mm(work[:, m * 2 * P:(m + 1) * 2 * P], wqkvo[:, w, c, m * P:(m + 1) * P], src[:, c, :],
                               start=(c == 0), stop=(c == DC - 1))
                i.then_inc(done, 1)

            def project_k(j):
                pe.wait_ge(ctx_loaded, 16 * j + 16)
                project(1, ctxT, k_ps)

            def project_q(j):
                pe.wait_ge(xnT_ready, j + 1)
                project(0, xnT, q_ps)

            def project_v(j):
                for b in range(2):
                    for c in range(DC):
                        i = mm(work[:, b * D:(b + 1) * D], ctxT[:, c, b * CTX:(b + 1) * CTX], wqkvo[:, 2, c, :],
                               start=(c == 0), stop=(c == DC - 1))
                i.then_inc(v_ps, 1)

            def scores(j, u):
                b, m = divmod(u, 2)
                n = 4 * j + u
                pe.wait_ge(kblk_ready, n + 1)
                if u == 0:
                    pe.wait_ge(qT_ready, j + 1)
                if not (isinstance(n, int) and n < 2):
                    pe.wait_ge(exps_done, n - 1)
                for hb in range(2):
                    i = mm(big[:, u % 2, hb, :], qT[:, m, b * P:(b + 1) * P],
                           kblk[:, u % 2, 4 * hb:4 * hb + 4, :].rearrange("p h k -> p (h k)"), start=True, stop=True)
                i.then_inc(scores_ready, 1)

            def transpose_probs(j, u):
                n = 4 * j + u
                pe.wait_ge(probs_ready, n + 1)
                for g in range(2):
                    if not (isinstance(n, int) and n < 1):
                        pe.wait_ge(pt_copied, 2 * n - 1 + g)
                    for h in range(4):
                        i = tr(mid[:, g, h * P:(h + 1) * P], probs[:, u % 2, 4 * g + h, :], ident)
                    i.then_inc(pt_ready, 1)

            def weigh_values(j, u):
                n = 4 * j + u
                pe.wait_ge(v_ready, n + 1)
                if not (isinstance(n, int) and n < 1):
                    pe.wait_ge(heads_copied, n)
                for h in range(HG):
                    if h % 4 == 0:
                        pe.wait_ge(pt_copied, 2 * n + h // 4 + 1)
                    i = mm(last[:, 0:P], vmask[:, u, h * P:(h + 1) * P], pT[:, h // 4, h % 4, :],
                           start=(h == 0), stop=(h == HG - 1))
                i.then_inc(av_ready, 1)

            def project_out(j, b):
                pe.wait_ge(heads_copied, 4 * j + 2 * b + 2)
                for m in range(DC):
                    i = mm(work[:, 0:D], outT[:, 2 * b + m, :], wqkvo[:, 3, m, :], start=(m == 0), stop=(m == DC - 1))
                i.then_inc(o_ps, 1)

            def transpose_xf(j):
                pe.wait_ge(xf_ready, 2 * j + 2)
                for b in range(2):
                    for c in range(DC):
                        i = tr(work[:, (2 * c + b) * P:(2 * c + b + 1) * P], xfs[:, b, c * P:(c + 1) * P], ident)
                i.then_inc(xfT_ps, 1)

            def router(j):
                pe.wait_ge(xfT_ready, j + 1)
                for b in range(2):
                    for c in range(DC):
                        i = mm(work[:, b * P:(b + 1) * P], xfT[:, c, b * P:(b + 1) * P], wg_pad[:, c, :],
                               start=(c == 0), stop=(c == DC - 1))
                i.then_inc(lg_ps, 1)

            def pair(j, ahead, ahead2, behind):
                for u in range(UNITS):
                    transpose_probs(j, u)
                    if behind:
                        if u == 0:
                            pe.wait_ge(xnT_ready, j + 2) if ahead else pe.wait_ge(lg_taken, j - 1)
                            project_out(j - 1, 0)
                        if u == 1:
                            pe.wait_ge(kT_ready, j + 2) if ahead else pe.wait_ge(o_taken, 2 * j - 1)
                            project_out(j - 1, 1)
                        if u == 2:
                            pe.wait_ge(qT_ready, j + 2) if ahead else pe.wait_ge(o_taken, 2 * j)
                            transpose_xf(j - 1)
                        if u == 3:
                            if ahead:
                                pe.wait_ge(v_copied, j + 2)
                            router(j - 1)
                    if u < 2:
                        scores(j, u + 2)
                    elif ahead:
                        scores(j + 1, u - 2)
                    if ahead:
                        if u == 0:
                            pe.wait_ge(o_taken, 2 * j - 1) if behind else pe.wait_ge(xnT_ready, j + 2)
                            project_k(j + 1)
                        if u == 1:
                            pe.wait_ge(o_taken, 2 * j) if behind else pe.wait_ge(kT_ready, j + 2)
                            project_q(j + 1)
                        if u == 2:
                            pe.wait_ge(xfT_ready, j) if behind else pe.wait_ge(qT_ready, j + 2)
                            project_v(j + 1)
                    if ahead2 and u == 3:
                        pe.wait_ge(lg_taken, j) if behind else pe.wait_ge(v_copied, j + 2)
                        project_xnT(j + 2)
                    weigh_values(j, u)

            pe.wait_ge(const_loaded, 16)
            project_xnT(0)
            pe.wait_ge(attn_w_loaded, 16)
            pe.wait_ge(xnT_ready, 1)
            project_k(0)
            pe.wait_ge(kT_ready, 1)
            project_q(0)
            pe.wait_ge(qT_ready, 1)
            project_v(0)
            scores(0, 0)
            pe.wait_ge(v_copied, 1)
            project_xnT(1)
            scores(0, 1)
            pe.wait_ge(wg_loaded, 16)
            pair(0, True, True, False)
            with pe.Fori(1, LAST - 1) as j:
                pair(j, True, True, True)
            pair(LAST - 1, True, False, True)
            pair(LAST, False, False, True)
            def shared_up(g, c):
                n = SC * g + c
                if n >= 2:
                    pe.wait_ge(gsh_ready, n - 1)
                for w, wt in enumerate((ws1, ws11)):
                    for k in range(DC):
                        i = mm(big[:, c % 2, w, :], wt[:, k, c * P:(c + 1) * P],
                               xfT_all[:, k, GROUP * P * g:GROUP * P * (g + 1)], start=(k == 0), stop=(k == DC - 1))
                i.then_inc(sh_ps, 1)

            def shared_down(g):
                for t in range(GROUP):
                    n = GROUP * g + t
                    if n >= 2:
                        pe.wait_ge(z_taken, n - 1)
                    for c in range(SC):
                        if t == 0:
                            pe.wait_ge(gsh_ready, SC * g + c + 1)
                        i = mm(zbank[t % 2][:, 0:D], gshT[:, c, t * P:(t + 1) * P], ws2[:, c, :], start=(c == 0), stop=(c == SC - 1))
                    i.then_inc(z_ps, 1)

            pe.wait_ge(lg_taken, LAST)
            project_out(LAST, 0)
            pe.wait_ge(shared_loaded, 16)
            pe.wait_ge(xfT_kept, 2)
            shared_up(0, 0)
            pe.wait_ge(o_taken, 2 * LAST + 1)
            project_out(LAST, 1)
            shared_up(0, 1)
            pe.wait_ge(o_taken, 2 * LAST + 2)
            transpose_xf(LAST)
            shared_up(0, 2)
            router(LAST)
            shared_up(0, 3)
            shared_up(0, 4)
            pe.wait_ge(onehots_ready, 1)
            mm(mid[:, 0, 0:TILES * E], const[:, C_TRI:C_TRI + P], rt[:, 0, :], start=True, stop=True)
            mm(mid[:, 1, 0:TILES * E], const[:, C_ONE:C_ONE + P], rt[:, 0, :], start=True, stop=True).then_inc(rank_ps, 1)
            for c in range(5, SC):
                shared_up(0, c)
            shared_down(0)
            pe.wait_ge(xfT_kept, PAIRS)
            for c in range(SC):
                shared_up(1, c)

            def expert_of(b):
                return pe.value_load(blk_expert[0:1, bass.ds(b, 1)], min_val=0, max_val=E - 1)

            def transpose_rows(b, q):
                pe.wait_ge(xs_loaded[q], 4 * (b - q) + 16)
                if not (isinstance(b, int) and b < 1):
                    pe.wait_ge(xsT_ready, b)
                for c in range(DC):
                    i = tr(work[:, c * P:(c + 1) * P], xs[:, q, c * P:(c + 1) * P], ident)
                i.then_inc(xs_ps, 1)

            def up(b, p):
                e = expert_of(b)
                slot = pe.snap(e % WSLOTS)
                pe.wait_ge(w_even, pe.snap(32 * (e // 2) + 32))
                pe.wait_ge(w_odd, pe.snap(32 * ((e + 1) // 2) + 16))
                pe.wait_ge(xsT_ready, b + 1)
                if not (isinstance(b, int) and b < 2):
                    pe.wait_ge(h_taken, b - 1)
                for w in range(2):
                    for k in range(DC):
                        i = mm(big[:, p, w, :], xsT[:, p, k, :],
                               ring[:, slot, (w * DC + k) * HID:(w * DC + k + 1) * HID], start=(k == 0), stop=(k == DC - 1))
                i.then_inc(up_ps, 1)

            def transpose_hidden(b, p):
                pe.wait_ge(g_ready, b + 1)
                if not (isinstance(b, int) and b < 1):
                    pe.wait_ge(gT_ready, b)
                for c in range(HC):
                    i = tr(mid[:, 0, c * P:(c + 1) * P], gg[:, p, c * P:(c + 1) * P], ident)
                i.then_inc(gt_ps, 1)

            def down(b, p):
                slot = pe.snap(expert_of(b) % WSLOTS)
                pe.wait_ge(gT_ready, b + 1)
                if not (isinstance(b, int) and b < 1):
                    pe.wait_ge(y_ready, b)
                for c in range(HC):
                    o = 2 * DC * HID + c * D
                    i = mm(mid[:, 1, 0:D], gT[:, p, c, :], ring[:, slot, o:o + D], start=(c == 0), stop=(c == HC - 1))
                i.then_inc(down_ps, 1)

            pe.wait_ge(table_ready, 1)
            pe.wait_ge(rank_taken, 1)
            pe.wait_ge(z_taken, GROUP)

            def slot(n, q, rows, ahead):
                p = q % 2
                if ahead:
                    up(n + 1, 1 - p)
                if rows:
                    transpose_rows(n + 3, (q + 3) % XBUFS)
                transpose_hidden(n, p)
                down(n - 1, 1 - p)

            transpose_rows(0, 0)
            transpose_rows(1, 1)
            pe.wait_ge(xsT_ready, 2)
            shared_down(1)
            up(0, 0)
            pe.wait_ge(z_taken, 2 * GROUP)
            transpose_rows(2, 2)
            up(1, 1)
            transpose_rows(3, 3)
            transpose_hidden(0, 0)
            for n in range(1, 5):
                slot(n, n % XBUFS, True, True)
            with pe.Fori(1, LOOPED // 4) as i:
                for q in range(1, 5):
                    slot(4 * i + q, q % XBUFS, True, True)
            for n in range(LOOPED + 1, BLOCKS - 1):
                slot(n, n % XBUFS, n + 3 < BLOCKS, True)
            pe.wait_ge(h_taken, BLOCKS)
            shared_up(2, 0)
            transpose_hidden(BLOCKS - 1, (BLOCKS - 1) % 2)
            down(BLOCKS - 2, BLOCKS % 2)
            shared_up(2, 1)
            down(BLOCKS - 1, (BLOCKS - 1) % 2)
            for c in range(2, SC):
                shared_up(2, c)
            shared_down(2)
            for c in range(SC):
                shared_up(3, c)
            shared_down(3)

        @block.scalar
        def _(act):
            act.wait_ge(gate_in_loaded, 32)
            nc.scalar.activation(tanh_g[:, :], gates_in[:, :], ACT.Tanh).then_inc(tanh_ready, 1)

            def exps(j, u):
                n = 4 * j + u
                act.wait_ge(negmax_ready, n + 1)
                if not (isinstance(n, int) and n < 2):
                    act.wait_ge(pt_ready, 2 * n - 2)
                for h in range(HG):
                    i = nc.scalar.activation(probs[:, u % 2, h, :], big[:, u % 2, h // 4, (h % 4) * CTX:(h % 4 + 1) * CTX],
                                             ACT.Exp, bias=nmax[:, u % 2, h:h + 1], accum_out=rsum[:, u % 2, h:h + 1])
                i.then_inc(exps_done, 1)

            def copy_probs(j, u):
                n = 4 * j + u
                if not (isinstance(n, int) and n < 1):
                    act.wait_ge(av_ready, n)
                for g in range(2):
                    act.wait_ge(pt_ready, 2 * n + g + 1)
                    nc.scalar.activation(pT[:, g, :, :].rearrange("p h q -> p (h q)"), mid[:, g, :], ACT.Copy) \
                        .then_inc(pt_copied, 1)

            def copy_heads(j, u):
                n = 4 * j + u
                act.wait_ge(av_ready, n + 1)
                nc.scalar.activation(outT[:, u, :], last[:, 0:P], ACT.Identity, bias=bias[:, B_V + u % 2:B_V + u % 2 + 1]) \
                    .then_inc(heads_copied, 1)

            def load_context(j):
                act.wait_ge(v_ps, j)
                act.dma_start(ctxT, ctx_t[j]).then_inc(ctx_loaded, 16)

            def pair(j, ahead, ahead2):
                for u in range(UNITS):
                    copy_probs(j, u)
                    if u < 2:
                        exps(j, u + 2)
                    elif ahead:
                        exps(j + 1, u - 2)
                    copy_heads(j, u)
                    if u == 2 and ahead2:
                        load_context(j + 2)

            act.wait_ge(bias_loaded, 16)
            load_context(1)
            exps(0, 0)
            exps(0, 1)
            pair(0, True, True)
            with act.Fori(1, LAST - 1) as j:
                pair(j, True, True)
            pair(LAST - 1, True, False)
            pair(LAST, False, False)

            def shared_silu(g, c):
                n = SC * g + c
                act.wait_ge(sh_ps, n + 1)
                if n >= 2:
                    act.wait_ge(gsh_ready, n - 1)
                nc.scalar.activation(sil[:, c % 2, :], big[:, c % 2, 0, :], ACT.Silu, bias=bias[:, B_S1 + c:B_S1 + c + 1]) \
                    .then_inc(silu_ready, 1)

            for g in range(2):
                for c in range(SC):
                    shared_silu(g, c)
            act.wait_ge(gate_exp_in, 1)
            nc.scalar.activation(gtmp[:, 1, :], gtmp[:, 0, :], ACT.Exp).then_inc(gate_exp, 1)

            def silu(b, p):
                act.wait_ge(h1_ready, b + 1)
                if not (isinstance(b, int) and b < 2):
                    act.wait_ge(g_ready, b - 1)
                nc.scalar.activation(sl[:, p, :], hb1[:, p, :], ACT.Silu).then_inc(s_ready, 1)

            def copy_hidden(b, p):
                act.wait_ge(gt_ps, b + 1)
                if not (isinstance(b, int) and b < 2):
                    act.wait_ge(down_ps, b - 1)
                nc.scalar.activation(gT[:, p, :, :].rearrange("p c n -> p (c n)"), mid[:, 0, :], ACT.Copy).then_inc(gT_ready, 1)

            def slot(n, p, ahead):
                if ahead:
                    silu(n + 1, 1 - p)
                copy_hidden(n, p)

            silu(0, 0)
            silu(1, 1)
            copy_hidden(0, 0)
            for n in range(1, 5):
                slot(n, n % 2, True)
            with act.Fori(1, LOOPED // 4) as i:
                for q in range(1, 5):
                    slot(4 * i + q, q % 2, True)
            for n in range(LOOPED + 1, BLOCKS):
                slot(n, n % 2, n + 1 < BLOCKS)
            for g in (2, 3):
                for c in range(SC):
                    shared_silu(g, c)
            for t in range(TILES):
                act.wait_ge(combined, t + 1)
                act.wait_ge(z_added, t + 1)
                act.dma_start(out[:, t, :], x_all[:, t, :]).then_inc(stored, 16)
            act.wait_ge(stored, 16 * TILES)

        @block.vector
        def _(dve):
            v = nc.vector
            links = [0, 0]
            base = [0]

            def link(ins):
                links[0] += 1
                ins.then_inc(dve_step, 1)
                dve.wait_ge(dve_step, base[0] + links[0])

            def carry():
                v.memset(carrier[:, :], 0.0)

            def norm_var(src, mv, ve, b, done):
                carry()
                link(v.bn_stats(stats[:, b, :], src))
                carry()
                link(v.bn_aggr(mv[:, b, :], stats[:, b, :]))
                v.tensor_scalar(ve[:, b:b + 1], mv[:, b, 1:2], EPS, None, ALU.add).then_inc(done, 1)

            def ln1_stats(j, b):
                norm_var(x_all[:, 2 * j + b, :], mv1, ve1, b, ln1_var)

            def ln1_apply(j, b):
                dve.wait_ge(ln1_rstd, 2 * j + b + 1)
                if not (isinstance(j, int) and j < 1):
                    dve.wait_ge(xnT_ps, j)
                v.tensor_scalar(xn[:, b, :], x_all[:, 2 * j + b, :], mv1[:, b, 0:1], rs1[:, b:b + 1],
                                ALU.subtract, ALU.mult).then_inc(xn_ready, 1)

            def add_attention(j, b):
                n = 2 * j + b
                dve.wait_ge(o_ps, n + 1)
                ins = v.tensor_tensor(att[:, :], work[:, 0:D], bo_bc, ALU.add)
                ins.then_inc(o_taken, 1)
                dve.wait_ge(o_taken, n + 1)
                link(v.scalar_tensor_tensor(out=x_all[:, n, :], in0=att[:, :], scalar=tanh_g[:, 0:1], in1=x_all[:, n, :],
                                            op0=ALU.mult, op1=ALU.add))
                norm_var(x_all[:, n, :], mv2, ve2, b, ln2_var)

            def ln2_apply(j, b):
                n = 2 * j + b
                dve.wait_ge(ln2_rstd, n + 1)
                if not (isinstance(j, int) and j < 1):
                    dve.wait_ge(xf_kept, 2 * j)
                v.tensor_scalar(xfs[:, b, :], x_all[:, n, :], mv2[:, b, 0:1], rs2[:, b:b + 1],
                                ALU.subtract, ALU.mult).then_inc(xf_ready, 1)

            def row_max(j, u):
                n = 4 * j + u
                dve.wait_ge(scores_ready, n + 1)
                link(v.reduce_max(rmax[:, u % 2, :], big[:, u % 2, :, :].rearrange("p a (h k) -> p (a h) k", k=CTX), AX.X))
                v.tensor_scalar(nmax[:, u % 2, :], rmax[:, u % 2, :], -1.0, None, ALU.mult).then_inc(negmax_ready, 1)

            def row_inv(j, u):
                n = 4 * j + u
                dve.wait_ge(exps_done, n + 1)
                if not (isinstance(n, int) and n < 2):
                    dve.wait_ge(probs_ready, n - 1)
                v.reciprocal(rinv[:, u % 2, :], rsum[:, u % 2, :]).then_inc(rinv_ready, 1)

            def copy_xnT(j):
                dve.wait_ge(xnT_ps, j + 1)
                if not (isinstance(j, int) and j < 1):
                    dve.wait_ge(q_ps, j)
                v.tensor_copy(xnT.rearrange("p c n -> p (c n)"), work[:, :]).then_inc(xnT_ready, 1)

            def copy_k(j):
                dve.wait_ge(k_ps, j + 1)
                if not (isinstance(j, int) and j < 1):
                    dve.wait_ge(kblk_ready, 4 * j)
                for m in range(DC):
                    i = v.tensor_scalar(kT[:, m, :], work[:, m * 2 * P:(m + 1) * 2 * P], bias[:, B_K + m:B_K + m + 1], None, ALU.add)
                i.then_inc(kT_ready, 1)

            def copy_q(j):
                dve.wait_ge(q_ps, j + 1)
                if not (isinstance(j, int) and j < 1):
                    dve.wait_ge(scores_ready, 4 * j)
                for m in range(DC):
                    i = v.tensor_scalar(qT[:, m, :], work[:, m * 2 * P:(m + 1) * 2 * P], bias[:, B_Q + m:B_Q + m + 1], SCALE,
                                        ALU.add, ALU.mult)
                i.then_inc(qT_ready, 1)

            def copy_v(j):
                dve.wait_ge(v_ps, j + 1)
                if not (isinstance(j, int) and j < 1):
                    dve.wait_ge(v_ready, 4 * j)
                v.tensor_copy(vflat.rearrange("p u c -> p (u c)"), work[:, :]).then_inc(v_copied, 1)

            def spread_values(j, u):
                dve.wait_ge(v_copied, j + 1)
                if not (isinstance(j, int) and j < 1):
                    dve.wait_ge(av_ready, 4 * j - 3 + u)
                v.tensor_copy(vmask[:, u, :].rearrange("p (h c) -> p h c", h=HG)[:, :, 0:DH],
                              vflat[:, u, :].rearrange("p (h c) -> p h c", h=HG)).then_inc(v_ready, 1)

            def copy_xfT(j):
                dve.wait_ge(xfT_ps, j + 1)
                if not (isinstance(j, int) and j < 1):
                    dve.wait_ge(lg_ps, j)
                    dve.wait_ge(xfT_kept, j)
                v.tensor_copy(xfT[:, :, :].rearrange("p c n -> p (c n)"), work[:, :]).then_inc(xfT_ready, 1)

            def choose_copy(j):
                dve.wait_ge(lg_ps, j + 1)
                v.tensor_copy(logits[:, :, :], work[:, 0:2 * P].rearrange("p (b e) -> p b e", b=2)[:, :, 0:E]) \
                    .then_inc(lg_taken, 1)

            def choose(j):
                dve.wait_ge(lg_taken, j + 1)
                carry()
                for b in range(2):
                    ins = v.max(top8[:, b, :], logits[:, b, :])
                link(ins)
                carry()
                for b in range(2):
                    ins = v.max_index(idx8[:, b, :], top8[:, b, :], logits[:, b, :])
                link(ins)
                link(v.tensor_copy(idxf[:, :, :], idx8[:, :, 0:TOPK]))
                for b in range(2):
                    for k in range(TOPK):
                        v.tensor_scalar(chosen[:, k, 2 * j + b, :], const[:, C_IE:C_IE + E], idxf[:, b, k:k + 1], None, ALU.is_equal)
                        ins = v.tensor_copy(top2[:, k, bass.ds(2 * j + b, 1)], top8[:, b, k:k + 1])
                link(ins)

            def pair(j, ahead, behind, ahead2):
                for u in range(UNITS):
                    if u < UNITS - 1:
                        row_inv(j, u + 1)
                    elif ahead:
                        row_inv(j + 1, 0)
                    if u == 0 and not (isinstance(j, int) and j < 1):
                        spread_values(j, UNITS - 1)
                    if u == 3 and ahead:
                        for w in range(UNITS - 1):
                            spread_values(j + 1, w)
                    if behind and u < 2:
                        add_attention(j - 1, u)
                    if behind and u == 2:
                        copy_xfT(j - 1)
                    if behind and u == 3:
                        choose_copy(j - 1)
                    if u < 2:
                        row_max(j, u + 2)
                    elif ahead:
                        row_max(j + 1, u - 2)
                    if ahead2 and u == 2:
                        for b in range(2):
                            ln1_stats(j + 2, b)
                    if ahead and u < 3:
                        (copy_k, copy_q, copy_v)[u](j + 1)
                    if ahead2 and u == 3:
                        copy_xnT(j + 2)
                    if behind and u < 2:
                        ln2_apply(j - 1, u)
                    if ahead2 and u == 2:
                        for b in range(2):
                            ln1_apply(j + 2, b)
                    if behind and u == 3:
                        choose(j - 1)

            v.memset(mhalf[:, :], -0.5).then_inc(half_ready, 1)
            v.memset(wg_pad[:, :, :], 0.0).then_inc(wg_zero, 1)
            dve.wait_ge(x_head_loaded, 16)
            for b in range(2):
                ln1_stats(0, b)
            for b in range(2):
                ln1_apply(0, b)
            for b in range(2):
                ln1_stats(1, b)
            dve.wait_ge(const_loaded, 16)
            copy_xnT(0)
            for b in range(2):
                ln1_apply(1, b)
            dve.wait_ge(bias_loaded, 16)
            copy_k(0)
            copy_q(0)
            copy_v(0)
            row_max(0, 0)
            copy_xnT(1)
            row_max(0, 1)
            dve.wait_ge(vmask_zero, 1)
            for u in range(UNITS):
                spread_values(0, u)
            row_inv(0, 0)
            dve.wait_ge(x_loaded, 16)
            dve.wait_ge(bo_loaded, 16)
            dve.wait_ge(tanh_ready, 1)
            pair(0, True, False, True)
            pair(1, True, True, True)
            before = links[0]
            LINKS = UNITS + 2 * 3 + 2 * 2 + 4
            with dve.Fori(2, LAST - 1) as j:
                base[0] = (j - 2) * LINKS
                pair(j, True, True, True)
            assert links[0] - before == LINKS, links[0] - before
            base[0] = (LAST - 4) * LINKS
            pair(LAST - 1, True, True, False)
            pair(LAST, False, True, False)
            def copy_rows(b, p):
                dve.wait_ge(xs_ps, b + 1)
                if not (isinstance(b, int) and b < 2):
                    dve.wait_ge(up_ps, b - 1)
                v.tensor_copy(xsT[:, p, :, :].rearrange("p c n -> p (c n)"), work[:, 0:D]).then_inc(xsT_ready, 1)

            def shared_hidden(g, chunks):
                for c in chunks:
                    n = SC * g + c
                    dve.wait_ge(silu_ready, n + 1)
                    if g > 0:
                        dve.wait_ge(z_ps, GROUP * g)
                    v.scalar_tensor_tensor(out=gshT[:, c, :], in0=big[:, c % 2, 1, :], scalar=bias[:, B_S11 + c:B_S11 + c + 1],
                                           in1=sil[:, c % 2, :], op0=ALU.add, op1=ALU.mult).then_inc(gsh_ready, 1)

            def add_shared(g):
                for t in range(GROUP):
                    n = GROUP * g + t
                    dve.wait_ge(z_ps, n + 1)
                    v.tensor_tensor(zt, zbank[t % 2][:, 0:D], bs2_bc[:, :], ALU.add).then_inc(z_taken, 1)
                    dve.wait_ge(z_taken, n + 1)
                    v.scalar_tensor_tensor(out=x_all[:, n, :], in0=zt, scalar=tanh_g[:, 1:2], in1=x_all[:, n, :],
                                           op0=ALU.mult, op1=ALU.add).then_inc(z_added, 1)
                    dve.wait_ge(z_added, n + 1)

            for b in range(2):
                add_attention(LAST, b)
                ln2_apply(LAST, b)
                shared_hidden(0, [b])
            copy_xfT(LAST)
            shared_hidden(0, [2])
            choose_copy(LAST)
            choose(LAST)

            def r3(i):
                return rt[:, i, :].rearrange("p (t e) -> p t e", t=TILES)

            ins = v.tensor_tensor(r3(0), chosen[:, 0, :, :], chosen[:, 1, :, :], ALU.add)
            ins.then_inc(onehots_ready, 1)
            v.tensor_tensor(gtmp[:, 0, :], top2[:, 1, :], top2[:, 0, :], ALU.subtract).then_inc(gate_exp_in, 1)
            shared_hidden(0, [3, 4])
            dve.wait_ge(rank_ps, 1)
            link(v.tensor_copy(rt[:, 1, :], mid[:, 1, 0:TILES * E]))
            cur, nxt, step = 1, 2, 1
            while step < TILES:
                v.tensor_copy(r3(nxt)[:, 0:step, :], r3(cur)[:, 0:step, :])
                link(v.tensor_tensor(r3(nxt)[:, step:, :], r3(cur)[:, step:, :], r3(cur)[:, :TILES - step, :], ALU.add))
                cur, nxt = nxt, 3 if nxt == 2 else 2
                step *= 2
            total = r3(cur)[:, TILES - 1, :]
            other = 2 if cur == 3 else 3
            cmp16 = blk_cmp[:, 0:TILES, :]
            link(v.tensor_tensor(cmp16, total.unsqueeze(1).to_broadcast([P, TILES, E]),
                                 const[:, C_IT:C_IT + TILES].unsqueeze(2).to_broadcast([P, TILES, E]), ALU.is_gt))
            link(v.tensor_reduce(cnt[:, 5, :], cmp16.rearrange("p t e -> p e t"), AX.X, ALU.add))
            link(v.tensor_scalar(cnt[:, 0, :], cnt[:, 5, :], 1.0, None, ALU.max))
            shared_hidden(0, [5])
            c_cur, c_nxt, step = 0, 1, 1
            while step < E:
                v.tensor_copy(cnt[:, c_nxt, 0:step], cnt[:, c_cur, 0:step])
                link(v.tensor_tensor(cnt[:, c_nxt, step:], cnt[:, c_cur, step:], cnt[:, c_cur, :E - step], ALU.add))
                c_cur, c_nxt = c_nxt, c_nxt + 1
                step *= 2
            ends = cnt[:, c_cur, :]
            v.tensor_copy(blk_end[:, :], ends)
            link(v.tensor_tensor(blk_cmp[:, :, :], ends.unsqueeze(1).to_broadcast([P, BLOCKS, E]),
                                 const[:, C_IB:C_IB + BLOCKS].unsqueeze(2).to_broadcast([P, BLOCKS, E]), ALU.is_le))
            link(v.tensor_reduce(blk_f[:, :], blk_cmp[:, :, :], AX.X, ALU.add))
            v.tensor_scalar(blk_expert[:, :], blk_f[:, :], float(E - 1), None, ALU.min).then_inc(table_ready, 1)
            link(v.tensor_tensor(cnt[:, 5, :], ends, cnt[:, 0, :], ALU.subtract))
            link(v.tensor_tensor(r3(other), r3(cur), r3(1), ALU.subtract))
            link(v.scalar_tensor_tensor(out=r3(cur), in0=cnt[:, 5, :].unsqueeze(1).to_broadcast([P, TILES, E]), scalar=float(P),
                                        in1=r3(other), op0=ALU.mult, op1=ALU.add))
            ins = v.tensor_tensor(r3(other), r3(cur), mid[:, 0, 0:TILES * E].rearrange("p (t e) -> p t e", t=TILES), ALU.add)
            ins.then_inc(rank_taken, 1)
            dve.wait_ge(rank_taken, 1)
            for k in range(TOPK):
                link(v.tensor_tensor(r3(0), chosen[:, k, :, :], r3(other), ALU.mult))
                link(v.tensor_reduce(pos_f[:, k, :], r3(0), AX.X, ALU.add))
            v.tensor_copy(pos[:, :, :], pos_f[:, :, :]).then_inc(pos_ready, 1)
            dve.wait_ge(w_odd, 16 + 32)
            shared_hidden(0, range(6, SC))
            add_shared(0)
            shared_hidden(1, range(SC))
            copy_rows(0, 0)
            copy_rows(1, 1)
            add_shared(1)
            dve.wait_ge(gate_exp, 1)
            link(v.tensor_scalar(gtmp[:, 2, :], gtmp[:, 1, :], 1.0, None, ALU.add))
            link(v.reciprocal(gtmp[:, 0, :], gtmp[:, 2, :]))
            link(v.tensor_scalar(gate[:, 0, :], gtmp[:, 0, :], tanh_g[:, 1:2], None, ALU.mult))
            v.tensor_tensor(gate[:, 1, :], gate[:, 0, :], gtmp[:, 1, :], ALU.mult).then_inc(gates_ready, 1)

            def slot_of(b):
                e = dve.value_load(blk_expert[0:1, bass.ds(b, 1)], min_val=0, max_val=E - 1)
                return dve.snap(e % WSLOTS)

            def add_biases(b, p):
                slot = slot_of(b)
                dve.wait_ge(up_ps, b + 1)
                if not (isinstance(b, int) and b < 2):
                    dve.wait_ge(s_ready, b - 1)
                    dve.wait_ge(g_ready, b - 1)
                v.tensor_tensor(hb1[:, p, :], big[:, p, 0, :], bring[:, slot, 0:HID], ALU.add).then_inc(h1_ready, 1)
                v.tensor_tensor(hb11[:, p, :], big[:, p, 1, :], bring[:, slot, HID:2 * HID], ALU.add).then_inc(h_taken, 1)

            def hidden(b, p):
                dve.wait_ge(s_ready, b + 1)
                dve.wait_ge(h_taken, b + 1)
                if not (isinstance(b, int) and b < 2):
                    dve.wait_ge(gt_ps, b - 1)
                v.tensor_tensor(gg[:, p, :], sl[:, p, :], hb11[:, p, :], ALU.mult).then_inc(g_ready, 1)

            def add_out_bias(b, p):
                slot = slot_of(b)
                dve.wait_ge(down_ps, b + 1)
                if not (isinstance(b, int) and b < 2):
                    dve.wait_ge(y_st_odd if p else y_st_even, 8 * (b - p))
                v.tensor_tensor(ysb[:, p, :], mid[:, 1, 0:D], bring[:, slot, 2 * HID:BCOLS], ALU.add).then_inc(y_ready, 1)

            dve.wait_ge(table_ready, 1)
            def slot(n, q, rows, ahead):
                p = q % 2
                if ahead:
                    add_biases(n + 1, 1 - p)
                if rows:
                    copy_rows(n + 3, 1 - p)
                if ahead:
                    hidden(n + 1, 1 - p)
                add_out_bias(n - 1, 1 - p)

            add_biases(0, 0)
            copy_rows(2, 0)
            hidden(0, 0)
            add_biases(1, 1)
            copy_rows(3, 1)
            hidden(1, 1)
            for n in range(1, 5):
                slot(n, n % XBUFS, True, True)
            with dve.Fori(1, LOOPED // 4) as i:
                for q in range(1, 5):
                    slot(4 * i + q, q % XBUFS, True, True)
            for n in range(LOOPED + 1, BLOCKS):
                slot(n, n % XBUFS, n + 3 < BLOCKS, n + 1 < BLOCKS)
            add_out_bias(BLOCKS - 1, (BLOCKS - 1) % 2)

            def combine(t):
                n = t % GATHERS
                dve.wait_ge(gathered_b if t >= GATHERS else gathered, 32 * GATHERS)
                link(v.scalar_tensor_tensor(out=x_all[:, t, :], in0=yg[:, n, 0, :], scalar=gate[:, 0, t:t + 1], in1=x_all[:, t, :],
                                            op0=ALU.mult, op1=ALU.add))
                v.scalar_tensor_tensor(out=x_all[:, t, :], in0=yg[:, n, 1, :], scalar=gate[:, 1, t:t + 1], in1=x_all[:, t, :],
                                       op0=ALU.mult, op1=ALU.add).then_inc(combined, 1)

            dve.wait_ge(gates_ready, 1)
            shared_hidden(2, range(SC))
            add_shared(2)
            for t in range(GATHERS):
                combine(t)
            shared_hidden(3, range(SC))
            for t in range(GATHERS, TILES):
                combine(t)
            add_shared(3)

        @block.gpsimd
        def _(pool):
            g = nc.gpsimd

            def rstd1(j, b):
                pool.wait_ge(ln1_var, 2 * j + b + 1)
                if not (isinstance(j, int) and j < 1):
                    pool.wait_ge(xn_ready, 2 * j)
                g.tensor_tensor(rs1[:, b:b + 1], ve1[:, b:b + 1], mhalf[:, :], ALU.pow).then_inc(ln1_rstd, 1)

            def rstd2(j, b):
                pool.wait_ge(ln2_var, 2 * j + b + 1)
                if not (isinstance(j, int) and j < 1):
                    pool.wait_ge(xf_ready, 2 * j)
                g.tensor_tensor(rs2[:, b:b + 1], ve2[:, b:b + 1], mhalf[:, :], ALU.pow).then_inc(ln2_rstd, 1)

            def spread_keys(j, u):
                b, m = divmod(u, 2)
                n = 4 * j + u
                if u == 0:
                    pool.wait_ge(kT_ready, j + 1)
                if not (isinstance(n, int) and n < 2):
                    pool.wait_ge(scores_ready, n - 1)
                g.tensor_tensor(kblk[:, u % 2, :, :],
                                kT[:, m, b * CTX:(b + 1) * CTX].unsqueeze(1).to_broadcast([P, HG, CTX]),
                                const[:, C_HM:C_HM + HG].unsqueeze(2).to_broadcast([P, HG, CTX]), ALU.mult) \
                    .then_inc(kblk_ready, 1)

            def normalise(j, u):
                n = 4 * j + u
                pool.wait_ge(rinv_ready, n + 1)
                g.tensor_tensor(probs[:, u % 2, :, :], probs[:, u % 2, :, :],
                                rinv[:, u % 2, :].unsqueeze(2).to_broadcast([P, HG, CTX]), ALU.mult).then_inc(probs_ready, 1)

            def keep_xf(j, b):
                pool.wait_ge(xf_ready, 2 * j + b + 1)
                g.tensor_copy(xf_all[:, 2 * j + b, :], xfs[:, b, :]).then_inc(xf_kept, 1)

            def keep_xfT(j):
                pool.wait_ge(xfT_ready, j + 1)
                g.tensor_copy(xfT_all[:, :, bass.ds(2 * P * j, 2 * P)], xfT[:, :, :]).then_inc(xfT_kept, 1)

            def pair(j, ahead, behind, ahead2):
                for u in range(UNITS):
                    if u < UNITS - 1:
                        normalise(j, u + 1)
                    elif ahead:
                        normalise(j + 1, 0)
                    if u == 0:
                        spread_keys(j, UNITS - 1)
                    elif ahead:
                        spread_keys(j + 1, u - 1)
                    if behind and u < 2:
                        rstd2(j - 1, u)
                    if ahead2 and u == 2:
                        for b in range(2):
                            rstd1(j + 2, b)
                    if behind and u in (1, 2):
                        keep_xf(j - 1, u - 1)
                    if behind and u == 3:
                        keep_xfT(j - 1)

            pool.wait_ge(half_ready, 1)
            g.memset(vmask, 0.0).then_inc(vmask_zero, 1)
            for b in range(2):
                rstd1(0, b)
            for b in range(2):
                rstd1(1, b)
            pool.wait_ge(const_loaded, 16)
            spread_keys(0, 0)
            spread_keys(0, 1)
            g.memset(ring[:, 2, :], 0.0).then_inc(xs_zero, 1)
            spread_keys(0, 2)
            normalise(0, 0)
            pair(0, True, False, True)
            pair(1, True, True, True)
            with pool.Fori(2, LAST - 1) as j:
                pair(j, True, True, True)
            pair(LAST - 1, True, True, False)
            pair(LAST, False, True, False)
            for b in range(2):
                rstd2(LAST, b)
            for b in range(2):
                keep_xf(LAST, b)
            keep_xfT(LAST)

            pool.wait_ge(pos_ready, 1)
            pool.wait_ge(xf_kept, TILES)
            pool.wait_ge(zeroed, 16 * ZDMAS)
            for t in range(TILES):
                for k in range(TOPK):
                    g.indirect_dma_start(out=sorted_x, out_offset=bass.IndirectOffsetOnAxis(ap=pos[:, k, t:t + 1], axis=0),
                                         in_=xf_all[:, t, :], in_offset=None).then_inc(scattered, 16)
            pool.wait_ge(scattered, 16 * TILES * TOPK)

            def load_rows(b, q):
                if not (isinstance(b, int) and b < XBUFS):
                    pool.wait_ge(xs_ps, b - XBUFS + 1)
                pool.dma_start(xs[:, q, :], sorted_x[bass.ds(b * P, P), :]).then_inc(xs_loaded[q], 16)

            def store_rows(b, p):
                pool.wait_ge(y_ready, b + 1)
                pool.dma_start(sorted_y[bass.ds(b * P, P), :], ysb[:, p, :]).then_inc(y_st_odd if p else y_st_even, 16)

            def slot(n, q, rows):
                if rows:
                    load_rows(n + AHEAD, (q + AHEAD) % XBUFS)
                store_rows(n - 1, (q + 1) % 2)

            for b in range(AHEAD + 1):
                load_rows(b, b % XBUFS)
            for n in range(1, 5):
                slot(n, n % XBUFS, True)
            with pool.Fori(1, LOOPED // 4) as i:
                for q in range(1, 5):
                    slot(4 * i + q, q % XBUFS, True)
            for n in range(LOOPED + 1, BLOCKS):
                slot(n, n % XBUFS, n + AHEAD < BLOCKS)
            store_rows(BLOCKS - 1, (BLOCKS - 1) % 2)
            pool.wait_ge(y_st_even, 16 * ((BLOCKS + 1) // 2))
            pool.wait_ge(y_st_odd, 16 * (BLOCKS // 2))
            for t in range(TILES):
                if t >= GATHERS:
                    pool.wait_ge(combined, t - GATHERS + 1)
                for k in range(TOPK):
                    g.indirect_dma_start(out=yg[:, t % GATHERS, k, :], out_offset=None, in_=sorted_y,
                                         in_offset=bass.IndirectOffsetOnAxis(ap=pos[:, k, t:t + 1], axis=0)) \
                        .then_inc(gathered_b if t >= GATHERS else gathered, 16)


def kernel(x, ctx_1024, g_xattn, g_ffn, L0_xattn_Wq, L0_xattn_bq, L0_xattn_Wk, L0_xattn_bk, L0_xattn_Wv, L0_xattn_bv,
           L0_xattn_Wo, L0_xattn_bo, L0_ffn_Wg, L0_ffn_W1, L0_ffn_b1, L0_ffn_W11, L0_ffn_b11, L0_ffn_W2, L0_ffn_b2,
           L0_ffn_Ws1, L0_ffn_bs1, L0_ffn_Ws11, L0_ffn_bs11, L0_ffn_Ws2, L0_ffn_bs2):
    import numpy as np
    import concourse.bacc as bacc
    from concourse.bass_utils import run_bass_kernel_spmd

    def rows(w):
        w = np.asarray(w)
        return w.reshape(w.shape[0] // P, P, w.shape[1]).transpose(1, 0, 2)

    def cols(v):
        return np.asarray(v).reshape(-1, P).T

    attn_w = np.stack([rows(np.asarray(w).T) for w in (L0_xattn_Wq, L0_xattn_Wk, L0_xattn_Wv, L0_xattn_Wo)], axis=1)
    col_bias = np.concatenate([cols(v) for v in (L0_xattn_bq, L0_xattn_bk, L0_xattn_bv, L0_ffn_bs1, L0_ffn_bs11)], axis=1)

    def expert_rows(w):
        w = np.asarray(w)
        return w.reshape(E, w.shape[1] // P, P, w.shape[2]).transpose(0, 2, 1, 3).reshape(E, P, -1)

    experts = np.concatenate([expert_rows(w) for w in (L0_ffn_W1, L0_ffn_W11, L0_ffn_W2)], axis=2)
    expert_bias = np.concatenate([np.asarray(b) for b in (L0_ffn_b1, L0_ffn_b11, L0_ffn_b2)], axis=1)
    shared_w = np.concatenate([rows(w).reshape(P, -1) for w in (L0_ffn_Ws1, L0_ffn_Ws11, L0_ffn_Ws2)], axis=1)

    i = np.arange(P)
    consts = np.zeros((P, CONSTS), np.float32)
    consts[:, C_ID:C_ID + P] = np.eye(P)
    consts[:, C_TRI:C_TRI + P] = i[:, None] < i[None, :]
    consts[:, C_ONE:C_ONE + P] = 1
    consts[:, C_HM:C_HM + HG] = i[:, None] // DH == np.arange(HG)[None, :]
    consts[:, C_IE:C_IE + E] = np.arange(E)
    consts[:, C_IB:C_IB + BLOCKS] = np.arange(BLOCKS)
    consts[:, C_IT:C_IT + TILES] = np.arange(TILES) * P

    ins = {
        "x": np.asarray(x).transpose(1, 0, 2),
        "ctx_t": np.asarray(ctx_1024).reshape(PAIRS, 2 * CTX, DC, P).transpose(0, 3, 2, 1),
        "attn_w": attn_w, "col_bias": col_bias, "bo": np.asarray(L0_xattn_bo),
        "g_xattn": np.asarray(g_xattn), "g_ffn": np.asarray(g_ffn), "w_gate": rows(L0_ffn_Wg),
        "experts": experts, "expert_bias": expert_bias, "shared_w": shared_w, "bs2": np.asarray(L0_ffn_bs2),
        "consts": consts,
    }
    nc = bacc.Bacc("TRN2", target_bir_lowering=False, num_devices=1)
    arrays, args = {}, []
    for name, a in ins.items():
        arrays[f"{name}_dram"] = a = np.ascontiguousarray(a)
        args.append(nc.dram_tensor(f"{name}_dram", a.shape, mybir.dt.from_np(a.dtype), kind="ExternalInput").ap())
    args.append(nc.dram_tensor("out_dram", (P, TILES, D), F32, kind="ExternalOutput").ap())
    flamingo_layer(nc, *args)
    r = run_bass_kernel_spmd(nc, [arrays], core_ids=[0])
    return np.ascontiguousarray(r.results[0]["out_dram"].transpose(1, 0, 2))
```

```python
from contextlib import ExitStack

import concourse.bass as bass
from concourse import mybir

P = 128
F32 = mybir.dt.float32
F32R = mybir.dt.float32r
I32 = mybir.dt.int32
U32 = mybir.dt.uint32
ALU = mybir.AluOpType
ACT = mybir.ActivationFunctionType
AX = mybir.AxisListType

TILES = 16
D = 256
DC = D // P
CTX = 128
NH = 16
DH = D // NH
HG = P // DH
E = 16
HID = 512
HC = HID // P
SHID = 1024
SC = SHID // P
HALVES = SHID // HID
EPS = 1e-5
SCALE = DH ** -0.5
PAIRS = TILES // 2
UNITS = 4
TOKENS = TILES * P
TOPK = 2
BLOCKS = (TOPK * TOKENS + E * (P - 1)) // P
ROWS = BLOCKS * P
XBUFS = 4
AHEAD = 6
LOOPED = (BLOCKS - 1 - AHEAD) // 4 * 4
ITEMS = E + 2
USLOTS = 2
WSLOTS = 3
UCOLS = 2 * DC * HID
DCOLS = HC * D
BCOLS = 2 * HID + D
ZROWS = WSLOTS * DCOLS // D
ZDMAS = -(-BLOCKS // ZROWS)
GROUP = 4
GATHERS = 8

C_ID, C_TRI, C_ONE, C_HM = 0, P, 2 * P, 3 * P
C_IE = C_HM + HG
C_IB = C_IE + E
C_IT = C_IB + BLOCKS
CONSTS = C_IT + TILES
B_Q, B_K, B_V, B_S1, B_S11 = 0, DC, 2 * DC, 3 * DC, 3 * DC + SC
BIASES = 3 * DC + 2 * SC


def flamingo_layer(nc, x, ctx_t, attn_w, col_bias, bo, g_xattn, g_ffn, w_gate, up_w, down_w, expert_bias,
                   bs2, consts, out):
    es = ExitStack()
    with es:
        def sb(name, shape, dt=F32):
            return es.enter_context(nc.sbuf_tensor(name, shape, dt))

        def sem(name):
            return es.enter_context(nc.semaphore(name))

        sorted_x = nc.dram_tensor("sorted_x", (ROWS, D), F32, kind="Internal").ap()
        sorted_y = nc.dram_tensor("sorted_y", (ROWS, D), F32, kind="Internal").ap()

        big = es.enter_context(nc.psum_tensor("big", [P, 2, 2, 512], F32))
        mid = es.enter_context(nc.psum_tensor("mid", [P, 2, 512], F32))
        work = es.enter_context(nc.psum_tensor("work", [P, 512], F32))
        last = es.enter_context(nc.psum_tensor("last", [P, 512], F32))

        zbank = (last, work)

        const = sb("const", [P, CONSTS])
        ident = const[:, C_ID:C_ID + P]
        bias = sb("bias", [P, BIASES])
        tanh_g = sb("tanh_g", [P, 2])
        gates_in = sb("gates_in", [P, 2])
        x_all = sb("x_all", [P, TILES, D])
        xf_all = sb("xf_all", [P, TILES, D])
        xfT_hi = sb("xfT_hi", [P, DC, TOKENS], F32R)
        xfT_lo = sb("xfT_lo", [P, DC, TOKENS], F32R)
        bs2_bc = sb("bs2_bc", [P, D])
        u_hi = sb("u_hi", [P, USLOTS, UCOLS], F32R)
        u_lo = sb("u_lo", [P, USLOTS, UCOLS], F32R)
        dring = sb("dring", [P, WSLOTS, DCOLS])
        bring = sb("bring", [P, WSLOTS, BCOLS])

        xsT_hi = sb("xsT_hi", [P, 2, D], F32R)
        xsT_lo = sb("xsT_lo", [P, 2, D], F32R)

        logits = sb("logits", [P, 2, E])
        top8 = sb("top8", [P, 2, 8])
        idx8 = sb("idx8", [P, 2, 8], U32)
        idxf = sb("idxf", [P, 2, 2])
        chosen = sb("chosen", [P, TOPK, TILES, E])
        top2 = sb("top2", [P, TOPK, TILES])
        cnt = sb("cnt", [P, 6, E])
        pos_f = sb("pos_f", [P, TOPK, TILES])
        pos = sb("pos", [P, TOPK, TILES], U32)
        gate = sb("gate", [P, TOPK, TILES])
        gtmp = sb("gtmp", [P, 3, TILES])
        blk_f = sb("blk_f", [P, BLOCKS])
        blk_item = sb("blk_item", [P, BLOCKS], I32)
        blk_end = sb("blk_end", [P, E], I32)

        ARENA = 16128
        arena = sb("arena", [P, ARENA])
        taken = [0]

        def part(cols):
            taken[0] += cols
            assert taken[0] <= ARENA, taken[0]
            return arena[:, taken[0] - cols:taken[0]]

        kblk = part(2 * HG * CTX).rearrange("p (s h k) -> p s h k", s=2, h=HG)
        probs = part(2 * HG * CTX).rearrange("p (s h k) -> p s h k", s=2, h=HG)
        pT = part(2 * 4 * P).rearrange("p (g h q) -> p g h q", g=2, h=4)
        wqkvo = part(4 * DC * D).rearrange("p (w c n) -> p w c n", w=4, c=DC)
        VB = HG * (P + DH)
        vmask = part(4 * VB).rearrange("p (u c) -> p u c", u=UNITS)
        xn = part(2 * D).rearrange("p (b n) -> p b n", b=2)
        xnT = part(DC * 2 * P).rearrange("p (c n) -> p c n", c=DC)
        ctxT = part(DC * 2 * CTX).rearrange("p (c n) -> p c n", c=DC)
        qT = part(DC * 2 * P).rearrange("p (c n) -> p c n", c=DC)
        kT = part(DC * 2 * CTX).rearrange("p (c n) -> p c n", c=DC)
        outT = part(UNITS * P).rearrange("p (u q) -> p u q", u=UNITS)
        vflat = part(2 * D).rearrange("p (u c) -> p u c", u=UNITS)
        bo_bc = part(D)
        taken[0] = 0
        gshT = part(2 * HC * 512).rearrange("p (s c n) -> p s c n", s=2, c=HC)
        sil = part(2 * 512).rearrange("p (s n) -> p s n", s=2)
        rt = part(4 * TILES * E).rearrange("p (i n) -> p i n", i=4)
        blk_cmp = part(BLOCKS * E).rearrange("p (b e) -> p b e", e=E)
        taken[0] -= (4 * TILES + BLOCKS) * E
        blocks_at = taken[0]
        hb1 = part(2 * HID).rearrange("p (s n) -> p s n", s=2)
        hb11 = part(2 * HID).rearrange("p (s n) -> p s n", s=2)
        sl = part(2 * HID).rearrange("p (s n) -> p s n", s=2)
        gg = part(2 * HID).rearrange("p (s n) -> p s n", s=2)
        gT = part(2 * HID).rearrange("p (s c n) -> p s c n", s=2, c=HC)
        xs = part(XBUFS * D).rearrange("p (s n) -> p s n", s=XBUFS)
        ysb = part(2 * D).rearrange("p (s n) -> p s n", s=2)
        zt = part(D)
        raw = part(2 * UCOLS).rearrange("p (s n) -> p s n", s=2)
        raw_first = dring[:, 1:WSLOTS, :].rearrange("p s n -> p (s n)")
        yg_a = xf_all[:, :, :].rearrange("p (t k) n -> p t k n", k=TOPK)
        yg_b = arena[:, blocks_at:blocks_at + GATHERS * TOPK * D].rearrange("p (t k n) -> p t k n", t=GATHERS, k=TOPK)

        xfs = sb("xfs", [P, 2, D])
        xfT = sb("xfT", [P, DC, 2 * P])
        wg_pad = sb("wg_pad", [P, DC, P])
        stats = sb("stats", [P, 2, 6])
        mv1 = sb("mv1", [P, 2, 2])
        mv2 = sb("mv2", [P, 2, 2])
        ve1 = sb("ve1", [P, 2])
        ve2 = sb("ve2", [P, 2])
        rs1 = sb("rs1", [P, 2])
        rs2 = sb("rs2", [P, 2])
        mhalf = sb("mhalf", [P, 1])
        carrier = sb("carrier", [P, 1])
        rmax = sb("rmax", [P, 2, HG])
        nmax = sb("nmax", [P, 2, HG])
        rsum = sb("rsum", [P, 2, HG])
        rinv = sb("rinv", [P, 2, HG])
        att = sb("att", [P, D])

        gT_ready = sem("gT_ready")
        kT_ready = sem("kT_ready")
        qT_ready = sem("qT_ready")
        xfT_kept = sem("xfT_kept")
        xfT_ps = sem("xfT_ps")
        xfT_ready = sem("xfT_ready")
        xnT_ps = sem("xnT_ps")
        xnT_ready = sem("xnT_ready")
        xsT_ready = sem("xsT_ready")
        const_loaded = sem("const_loaded")
        bias_loaded = sem("bias_loaded")
        x_head_loaded = sem("x_head_loaded")
        x_next_loaded = sem("x_next_loaded")
        x_loaded = sem("x_loaded")
        ctx_loaded = sem("ctx_loaded")
        qk_w_loaded = sem("qk_w_loaded")
        vo_w_loaded = sem("vo_w_loaded")
        gate_in_loaded = sem("gate_in_loaded")
        wg_loaded = sem("wg_loaded")
        bo_loaded = sem("bo_loaded")
        raw_first_loaded = sem("raw_first_loaded")
        raw_even = sem("raw_even")
        raw_odd = sem("raw_odd")
        hi_done = sem("hi_done")
        split_done = sem("split_done")
        xfT_hi_kept = sem("xfT_hi_kept")
        rows_hi = sem("rows_hi")
        zeroed = sem("zeroed")
        tanh_ready = sem("tanh_ready")
        wg_zero = sem("wg_zero")
        half_ready = sem("half_ready")
        vmask_zero = sem("vmask_zero")
        xs_zero = sem("xs_zero")
        dve_step = sem("dve_step")
        ln1_var = sem("ln1_var")
        ln1_rstd = sem("ln1_rstd")
        ln2_var = sem("ln2_var")
        ln2_rstd = sem("ln2_rstd")
        xn_ready = sem("xn_ready")
        k_ps = sem("k_ps")
        q_ps = sem("q_ps")
        v_ps = sem("v_ps")
        v_copied = sem("v_copied")
        v_ready = sem("v_ready")
        kblk_ready = sem("kblk_ready")
        scores_ready = sem("scores_ready")
        negmax_ready = sem("negmax_ready")
        exps_done = sem("exps_done")
        rinv_ready = sem("rinv_ready")
        probs_ready = sem("probs_ready")
        pt_ready = sem("pt_ready")
        pt_copied = sem("pt_copied")
        av_ready = sem("av_ready")
        heads_copied = sem("heads_copied")
        o_ps = sem("o_ps")
        o_taken = sem("o_taken")
        xf_ready = sem("xf_ready")
        xf_kept = sem("xf_kept")
        lg_ps = sem("lg_ps")
        lg_taken = sem("lg_taken")
        onehots_ready = sem("onehots_ready")
        rank_ps = sem("rank_ps")
        rank_taken = sem("rank_taken")
        table_ready = sem("table_ready")
        pos_ready = sem("pos_ready")
        gate_exp_in = sem("gate_exp_in")
        gate_exp = sem("gate_exp")
        scattered = sem("scattered")
        w_even = sem("w_even")
        w_odd = sem("w_odd")
        xs0_loaded = sem("xs0_loaded")
        xs1_loaded = sem("xs1_loaded")
        xs2_loaded = sem("xs2_loaded")
        xs3_loaded = sem("xs3_loaded")
        xs_loaded = (xs0_loaded, xs1_loaded, xs2_loaded, xs3_loaded)
        xs_ps = sem("xs_ps")
        up_ps = sem("up_ps")
        h1_ready = sem("h1_ready")
        h_taken = sem("h_taken")
        s_ready = sem("s_ready")
        g_ready = sem("g_ready")
        gt_ps = sem("gt_ps")
        down_ps = sem("down_ps")
        y_ready = sem("y_ready")
        y_st_even = sem("y_st_even")
        y_st_odd = sem("y_st_odd")
        sh_ps = sem("sh_ps")
        silu_ready = sem("silu_ready")
        gsh_ready = sem("gsh_ready")
        z_ps = sem("z_ps")
        z_taken = sem("z_taken")
        z_added = sem("z_added")
        gathered = sem("gathered")
        gathered_b = sem("gathered_b")
        combined = sem("combined")
        gates_ready = sem("gates_ready")
        stored = sem("stored")

        block = es.enter_context(nc.Block())
        LAST = PAIRS - 1

        @block.sync
        def _(sp):
            sp.dma_start(x_all[:, 0:2, :], x[:, 0:2, :]).then_inc(x_head_loaded, 16)
            sp.dma_start(const[:, :], consts).then_inc(const_loaded, 16)
            sp.dma_start(ctxT, ctx_t[0]).then_inc(ctx_loaded, 16)
            sp.dma_start(wqkvo[:, 0:2], attn_w[:, 0:2]).then_inc(qk_w_loaded, 16)
            sp.dma_start(bias[:, :], col_bias).then_inc(bias_loaded, 16)
            sp.dma_start(x_all[:, 2:4, :], x[:, 2:4, :]).then_inc(x_next_loaded, 16)
            sp.dma_start(wqkvo[:, 2:4], attn_w[:, 2:4]).then_inc(vo_w_loaded, 16)
            sp.dma_start(x_all[:, 4:TILES, :], x[:, 4:TILES, :]).then_inc(x_loaded, 16)
            sp.dma_start(bo_bc, bo.partition_broadcast(P)).then_inc(bo_loaded, 16)
            sp.dma_start(gates_in[:, 0:1], g_xattn.partition_broadcast(P)).then_inc(gate_in_loaded, 16)
            sp.dma_start(gates_in[:, 1:2], g_ffn.partition_broadcast(P)).then_inc(gate_in_loaded, 16)
            sp.wait_ge(wg_zero, 1)
            sp.dma_start(wg_pad[:, :, 0:E], w_gate).then_inc(wg_loaded, 16)

            def load_raw(i):
                sp.dma_start(raw[:, i % 2, :], up_w[i]).then_inc(raw_odd if i % 2 else raw_even, 16)

            def load_down(i):
                done = w_odd if i % 2 else w_even
                sp.dma_start(dring[:, i % WSLOTS, :], down_w[i]).then_inc(done, 16)
                if 0 < i <= E:
                    sp.dma_start(bring[:, i % WSLOTS, :], expert_bias[i - 1].partition_broadcast(P)).then_inc(done, 16)

            sp.wait_ge(exps_done, 1)
            sp.wait_ge(xs_zero, 1)
            for r in range(0, BLOCKS, ZROWS):
                n = min(ZROWS, BLOCKS - r)
                sp.dma_start(sorted_x[r * P:(r + n) * P, :].rearrange("(p t) n -> p t n", p=P),
                             dring[:, :, :].rearrange("p s (t n) -> p (s t) n", n=D)[:, 0:n, :]).then_inc(zeroed, 16)
            sp.wait_ge(ctx_loaded, 48)
            sp.wait_ge(zeroed, 16 * ZDMAS)
            sp.dma_start(raw_first, up_w[0]).then_inc(raw_first_loaded, 16)
            load_down(0)
            sp.dma_start(bs2_bc[:, :], bs2.partition_broadcast(P)).then_inc(w_even, 16)
            sp.wait_ge(o_taken, TILES)
            load_raw(1)
            load_raw(2)
            sp.wait_ge(split_done, 1)
            load_down(1)
            sp.wait_ge(w_even, 32)
            load_down(2)
            sp.wait_ge(scattered, 16 * TILES * TOPK)
            for b in range(XBUFS):
                sp.dma_start(xs[:, b, :], sorted_x[b * P:(b + 1) * P, :]).then_inc(xs_loaded[b], 16)
            sp.wait_ge(table_ready, 1)
            for i in range(3, ITEMS):
                sp.wait_ge(split_done, i - 1)
                load_raw(i)
                sp.wait_ge(w_odd if i % 2 else w_even, 32 * (i // 2))
                if i == 3:
                    sp.wait_ge(z_ps, TILES)
                else:
                    end = sp.value_load(blk_end[0:1, bass.ds(i - WSLOTS - 1, 1)], min_val=1, max_val=BLOCKS)
                    sp.wait_ge(y_ready, end)
                load_down(i)

        @block.tensor
        def _(pe):
            mm, tr = nc.tensor.matmul, nc.tensor.transpose

            def project_xnT(j, bank=work):
                pe.wait_ge(xn_ready, 2 * j + 2)
                for b in range(2):
                    for c in range(DC):
                        i = tr(bank[:, (2 * c + b) * P:(2 * c + b + 1) * P], xn[:, b, c * P:(c + 1) * P], ident)
                i.then_inc(xnT_ps, 1)

            def project(w, src, done, bank):
                for m in range(DC):
                    for c in range(DC):
                        i = mm(bank[:, m * 2 * P:(m + 1) * 2 * P], wqkvo[:, w, c, m * P:(m + 1) * P], src[:, c, :],
                               start=(c == 0), stop=(c == DC - 1))
                i.then_inc(done, 1)

            def project_k(j):
                pe.wait_ge(ctx_loaded, 16 * j + 16)
                project(1, ctxT, k_ps, work)

            def project_q(j, bank=work):
                pe.wait_ge(xnT_ready, j + 1)
                project(0, xnT, q_ps, bank)

            def project_v(j, bank=work):
                for b in range(2):
                    for c in range(DC):
                        i = mm(bank[:, b * D:(b + 1) * D], ctxT[:, c, b * CTX:(b + 1) * CTX], wqkvo[:, 2, c, :],
                               start=(c == 0), stop=(c == DC - 1))
                i.then_inc(v_ps, 1)

            def scores(j, u):
                b, m = divmod(u, 2)
                n = 4 * j + u
                pe.wait_ge(kblk_ready, n + 1)
                if u == 0:
                    pe.wait_ge(qT_ready, j + 1)
                if not (isinstance(n, int) and n < 2):
                    pe.wait_ge(exps_done, n - 1)
                for hb in range(2):
                    i = mm(big[:, u % 2, hb, :], qT[:, m, b * P:(b + 1) * P],
                           kblk[:, u % 2, 4 * hb:4 * hb + 4, :].rearrange("p h k -> p (h k)"), start=True, stop=True)
                i.then_inc(scores_ready, 1)

            def transpose_probs(j, u):
                n = 4 * j + u
                pe.wait_ge(probs_ready, n + 1)
                for g in range(2):
                    if not (isinstance(n, int) and n < 1):
                        pe.wait_ge(pt_copied, 2 * n - 1 + g)
                    for h in range(4):
                        i = tr(mid[:, g, h * P:(h + 1) * P], probs[:, u % 2, 4 * g + h, :], ident)
                    i.then_inc(pt_ready, 1)

            def weigh_values(j, u):
                n = 4 * j + u
                pe.wait_ge(v_ready, n + 1)
                if not (isinstance(n, int) and n < 1):
                    pe.wait_ge(heads_copied, n)
                for h in range(HG):
                    if h % 4 == 0:
                        pe.wait_ge(pt_copied, 2 * n + h // 4 + 1)
                    i = mm(last[:, 0:P], vmask[:, u, h * P:(h + 1) * P], pT[:, h // 4, h % 4, :],
                           start=(h == 0), stop=(h == HG - 1))
                i.then_inc(av_ready, 1)

            def project_out(j, b):
                pe.wait_ge(heads_copied, 4 * j + 2 * b + 2)
                for m in range(DC):
                    i = mm(work[:, 0:D], outT[:, 2 * b + m, :], wqkvo[:, 3, m, :], start=(m == 0), stop=(m == DC - 1))
                i.then_inc(o_ps, 1)

            def transpose_xf(j):
                pe.wait_ge(xf_ready, 2 * j + 2)
                for b in range(2):
                    for c in range(DC):
                        i = tr(work[:, (2 * c + b) * P:(2 * c + b + 1) * P], xfs[:, b, c * P:(c + 1) * P], ident)
                i.then_inc(xfT_ps, 1)

            def router(j):
                pe.wait_ge(xfT_ready, j + 1)
                for b in range(2):
                    for c in range(DC):
                        i = mm(work[:, b * P:(b + 1) * P], xfT[:, c, b * P:(b + 1) * P], wg_pad[:, c, :],
                               start=(c == 0), stop=(c == DC - 1))
                i.then_inc(lg_ps, 1)

            def pair(j, ahead, ahead2, behind):
                for u in range(UNITS):
                    transpose_probs(j, u)
                    if behind:
                        if u == 0:
                            pe.wait_ge(xnT_ready, j + 2) if ahead else pe.wait_ge(lg_taken, j - 1)
                            project_out(j - 1, 0)
                        if u == 1:
                            pe.wait_ge(kT_ready, j + 2) if ahead else pe.wait_ge(o_taken, 2 * j - 1)
                            project_out(j - 1, 1)
                        if u == 2:
                            pe.wait_ge(qT_ready, j + 2) if ahead else pe.wait_ge(o_taken, 2 * j)
                            transpose_xf(j - 1)
                        if u == 3:
                            if ahead:
                                pe.wait_ge(v_copied, j + 2)
                            router(j - 1)
                    if u < 2:
                        scores(j, u + 2)
                    elif ahead:
                        scores(j + 1, u - 2)
                    if ahead:
                        if u == 0:
                            pe.wait_ge(o_taken, 2 * j - 1) if behind else pe.wait_ge(xnT_ready, j + 2)
                            project_k(j + 1)
                        if u == 1:
                            pe.wait_ge(o_taken, 2 * j) if behind else pe.wait_ge(kT_ready, j + 2)
                            project_q(j + 1)
                        if u == 2:
                            pe.wait_ge(xfT_ready, j) if behind else pe.wait_ge(qT_ready, j + 2)
                            project_v(j + 1)
                    if ahead2 and u == 3:
                        pe.wait_ge(lg_taken, j) if behind else pe.wait_ge(v_copied, j + 2)
                        project_xnT(j + 2)
                    weigh_values(j, u)

            pe.wait_ge(const_loaded, 16)
            project_xnT(0, mid[:, 0, :])
            pe.wait_ge(qk_w_loaded, 16)
            project_k(0)
            project_q(0, last)
            pe.wait_ge(vo_w_loaded, 16)
            project_v(0, mid[:, 1, :])
            pe.wait_ge(kT_ready, 1)
            project_xnT(1)
            scores(0, 0)
            scores(0, 1)
            pe.wait_ge(v_copied, 1)
            pe.wait_ge(wg_loaded, 16)
            pair(0, True, True, False)
            with pe.Fori(1, LAST - 1) as j:
                pair(j, True, True, True)
            pair(LAST - 1, True, False, True)
            pair(LAST, False, False, True)
            def shared_up(s, c):
                h, g = divmod(s, TILES // GROUP)
                n = HC * s + c
                if n >= 2:
                    pe.wait_ge(gsh_ready, n - 1)
                slot = (ITEMS - 1) % USLOTS if h else 0
                x_hi = [xfT_hi[:, k, GROUP * P * g:GROUP * P * (g + 1)] for k in range(DC)]
                x_lo = [xfT_lo[:, k, GROUP * P * g:GROUP * P * (g + 1)] for k in range(DC)]
                for w in range(2):
                    for k in range(DC):
                        o = (w * DC + k) * HID + c * P
                        w_hi, w_lo = u_hi[:, slot, o:o + P], u_lo[:, slot, o:o + P]
                        mm(big[:, c % 2, w, :], w_hi, x_hi[k], start=(k == 0), stop=False)
                        mm(big[:, c % 2, w, :], w_hi, x_lo[k], start=False, stop=False)
                        i = mm(big[:, c % 2, w, :], w_lo, x_hi[k], start=False, stop=(k == DC - 1))
                i.then_inc(sh_ps, 1)

            def shared_ups(s):
                for c in range(HC):
                    shared_up(s, c)

            def shared_down(s, tiles=range(GROUP)):
                slot = (ITEMS - 1) % WSLOTS if s >= TILES // GROUP else 0
                for t in tiles:
                    n = GROUP * s + t
                    if n >= 2:
                        pe.wait_ge(z_taken, n - 1)
                    for c in range(HC):
                        if t == 0:
                            pe.wait_ge(gsh_ready, HC * s + c + 1)
                        i = mm(zbank[t % 2][:, 0:D], gshT[:, s % 2, c, t * P:(t + 1) * P], dring[:, slot, c * D:(c + 1) * D],
                               start=(c == 0), stop=(c == HC - 1))
                    i.then_inc(z_ps, 1)

            pe.wait_ge(lg_taken, LAST)
            project_out(LAST, 0)
            pe.wait_ge(split_done, 1)
            pe.wait_ge(xfT_kept, 2)
            shared_up(0, 0)
            pe.wait_ge(o_taken, 2 * LAST + 1)
            project_out(LAST, 1)
            shared_up(0, 1)
            pe.wait_ge(o_taken, 2 * LAST + 2)
            transpose_xf(LAST)
            shared_up(0, 2)
            router(LAST)
            shared_up(0, 3)
            pe.wait_ge(xfT_kept, 4)
            shared_up(1, 0)
            shared_up(1, 1)
            pe.wait_ge(onehots_ready, 1)
            mm(mid[:, 0, 0:TILES * E], const[:, C_TRI:C_TRI + P], rt[:, 0, :], start=True, stop=True)
            mm(mid[:, 1, 0:TILES * E], const[:, C_ONE:C_ONE + P], rt[:, 0, :], start=True, stop=True).then_inc(rank_ps, 1)
            shared_up(1, 2)
            shared_up(1, 3)
            pe.wait_ge(w_even, 32)
            shared_down(0)
            pe.wait_ge(xfT_kept, PAIRS)
            shared_ups(2)
            shared_down(1)
            shared_ups(3)
            shared_down(2)

            def item_of(b):
                return pe.value_load(blk_item[0:1, bass.ds(b, 1)], min_val=1, max_val=E)

            def transpose_rows(b, q):
                pe.wait_ge(xs_loaded[q], 4 * (b - q) + 16)
                if not (isinstance(b, int) and b < 1):
                    pe.wait_ge(xsT_ready, b)
                for c in range(DC):
                    i = tr(work[:, c * P:(c + 1) * P], xs[:, q, c * P:(c + 1) * P], ident)
                i.then_inc(xs_ps, 1)

            def up(b, p):
                item = item_of(b)
                slot = pe.snap(item % USLOTS)
                pe.wait_ge(split_done, pe.snap(item + 1))
                pe.wait_ge(w_even, pe.snap(32 * (item // 2) + 32))
                pe.wait_ge(w_odd, pe.snap(32 * ((item + 1) // 2)))
                pe.wait_ge(xsT_ready, b + 1)
                if not (isinstance(b, int) and b < 2):
                    pe.wait_ge(h_taken, b - 1)
                for w in range(2):
                    for k in range(DC):
                        o = (w * DC + k) * HID
                        x_hi, x_lo = xsT_hi[:, p, k * P:(k + 1) * P], xsT_lo[:, p, k * P:(k + 1) * P]
                        mm(big[:, p, w, :], x_hi, u_hi[:, slot, o:o + HID], start=(k == 0), stop=False)
                        mm(big[:, p, w, :], x_hi, u_lo[:, slot, o:o + HID], start=False, stop=False)
                        i = mm(big[:, p, w, :], x_lo, u_hi[:, slot, o:o + HID], start=False, stop=(k == DC - 1))
                i.then_inc(up_ps, 1)

            def transpose_hidden(b, p):
                pe.wait_ge(g_ready, b + 1)
                if not (isinstance(b, int) and b < 1):
                    pe.wait_ge(gT_ready, b)
                for c in range(HC):
                    i = tr(mid[:, 0, c * P:(c + 1) * P], gg[:, p, c * P:(c + 1) * P], ident)
                i.then_inc(gt_ps, 1)

            def down(b, p):
                slot = pe.snap(item_of(b) % WSLOTS)
                pe.wait_ge(gT_ready, b + 1)
                if not (isinstance(b, int) and b < 1):
                    pe.wait_ge(y_ready, b)
                for c in range(HC):
                    i = mm(mid[:, 1, 0:D], gT[:, p, c, :], dring[:, slot, c * D:(c + 1) * D], start=(c == 0), stop=(c == HC - 1))
                i.then_inc(down_ps, 1)

            pe.wait_ge(table_ready, 1)
            pe.wait_ge(rank_taken, 1)
            pe.wait_ge(z_taken, 3 * GROUP)

            def slot(n, q, rows, ahead):
                p = q % 2
                if ahead:
                    up(n + 1, 1 - p)
                if rows:
                    transpose_rows(n + 3, (q + 3) % XBUFS)
                transpose_hidden(n, p)
                down(n - 1, 1 - p)

            transpose_rows(0, 0)
            shared_down(3, range(1))
            transpose_rows(1, 1)
            up(0, 0)
            pe.wait_ge(xsT_ready, 2)
            shared_down(3, range(1, GROUP))
            pe.wait_ge(z_taken, 4 * GROUP)
            transpose_rows(2, 2)
            up(1, 1)
            transpose_rows(3, 3)
            transpose_hidden(0, 0)
            for n in range(1, 5):
                slot(n, n % XBUFS, True, True)
            with pe.Fori(1, LOOPED // 4) as i:
                for q in range(1, 5):
                    slot(4 * i + q, q % XBUFS, True, True)
            for n in range(LOOPED + 1, BLOCKS - 1):
                slot(n, n % XBUFS, n + 3 < BLOCKS, True)
            pe.wait_ge(h_taken, BLOCKS)
            pe.wait_ge(split_done, ITEMS)
            shared_up(4, 0)
            transpose_hidden(BLOCKS - 1, (BLOCKS - 1) % 2)
            down(BLOCKS - 2, BLOCKS % 2)
            shared_up(4, 1)
            down(BLOCKS - 1, (BLOCKS - 1) % 2)
            shared_up(4, 2)
            shared_up(4, 3)
            pe.wait_ge(w_odd, 32 * (ITEMS // 2 - 1) + 16)
            for s in range(5, 8):
                shared_ups(s)
                shared_down(s - 1)
            shared_down(7)

        @block.scalar
        def _(act):
            act.wait_ge(gate_in_loaded, 32)
            nc.scalar.activation(tanh_g[:, :], gates_in[:, :], ACT.Tanh).then_inc(tanh_ready, 1)

            def exps(j, u):
                n = 4 * j + u
                act.wait_ge(negmax_ready, n + 1)
                if not (isinstance(n, int) and n < 2):
                    act.wait_ge(pt_ready, 2 * n - 2)
                for h in range(HG):
                    i = nc.scalar.activation(probs[:, u % 2, h, :], big[:, u % 2, h // 4, (h % 4) * CTX:(h % 4 + 1) * CTX],
                                             ACT.Exp, bias=nmax[:, u % 2, h:h + 1], accum_out=rsum[:, u % 2, h:h + 1])
                i.then_inc(exps_done, 1)

            def copy_probs(j, u):
                n = 4 * j + u
                if not (isinstance(n, int) and n < 1):
                    act.wait_ge(av_ready, n)
                for g in range(2):
                    act.wait_ge(pt_ready, 2 * n + g + 1)
                    nc.scalar.activation(pT[:, g, :, :].rearrange("p h q -> p (h q)"), mid[:, g, :], ACT.Copy) \
                        .then_inc(pt_copied, 1)

            def copy_heads(j, u):
                n = 4 * j + u
                act.wait_ge(av_ready, n + 1)
                nc.scalar.activation(outT[:, u, :], last[:, 0:P], ACT.Identity, bias=bias[:, B_V + u % 2:B_V + u % 2 + 1]) \
                    .then_inc(heads_copied, 1)

            def load_context(j):
                act.wait_ge(v_ps, j)
                act.dma_start(ctxT, ctx_t[j]).then_inc(ctx_loaded, 16)

            def pair(j, ahead, ahead2):
                for u in range(UNITS):
                    copy_probs(j, u)
                    if u < 2:
                        exps(j, u + 2)
                    elif ahead:
                        exps(j + 1, u - 2)
                    copy_heads(j, u)
                    if u == 2 and ahead2:
                        load_context(j + 2)

            act.wait_ge(bias_loaded, 16)
            load_context(1)
            exps(0, 0)
            exps(0, 1)
            pair(0, True, True)
            with act.Fori(1, LAST - 1) as j:
                pair(j, True, True)
            pair(LAST - 1, True, False)
            pair(LAST, False, False)

            def shared_silu(s, c):
                n = HC * s + c
                o = B_S1 + HC * (s // (TILES // GROUP)) + c
                act.wait_ge(sh_ps, n + 1)
                if n >= 2:
                    act.wait_ge(gsh_ready, n - 1)
                nc.scalar.activation(sil[:, c % 2, :], big[:, c % 2, 0, :], ACT.Silu, bias=bias[:, o:o + 1]) \
                    .then_inc(silu_ready, 1)

            for s in range(4):
                for c in range(HC):
                    shared_silu(s, c)
            act.wait_ge(gate_exp_in, 1)
            nc.scalar.activation(gtmp[:, 1, :], gtmp[:, 0, :], ACT.Exp).then_inc(gate_exp, 1)

            def silu(b, p):
                act.wait_ge(h1_ready, b + 1)
                if not (isinstance(b, int) and b < 2):
                    act.wait_ge(g_ready, b - 1)
                nc.scalar.activation(sl[:, p, :], hb1[:, p, :], ACT.Silu).then_inc(s_ready, 1)

            def copy_hidden(b, p):
                act.wait_ge(gt_ps, b + 1)
                if not (isinstance(b, int) and b < 2):
                    act.wait_ge(down_ps, b - 1)
                nc.scalar.activation(gT[:, p, :, :].rearrange("p c n -> p (c n)"), mid[:, 0, :], ACT.Copy).then_inc(gT_ready, 1)

            def load_rows(b, q):
                act.wait_ge(xs_ps, b - XBUFS + 1)
                act.dma_start(xs[:, q, :], sorted_x[bass.ds(b * P, P), :]).then_inc(xs_loaded[q], 16)

            def store_rows(b, p):
                act.wait_ge(y_ready, b + 1)
                act.dma_start(sorted_y[bass.ds(b * P, P), :], ysb[:, p, :]).then_inc(y_st_odd if p else y_st_even, 16)

            def slot(n, q, rows, store, ahead):
                if rows:
                    load_rows(n + AHEAD, (q + AHEAD) % XBUFS)
                if ahead:
                    silu(n + 1, 1 - q % 2)
                copy_hidden(n, q % 2)
                if store:
                    store_rows(n - 2, q % 2)

            act.wait_ge(scattered, 16 * TILES * TOPK)
            load_rows(4, 0)
            load_rows(5, 1)
            silu(0, 0)
            load_rows(6, 2)
            silu(1, 1)
            copy_hidden(0, 0)
            for n in range(1, 5):
                slot(n, n % XBUFS, True, n > 1, True)
            with act.Fori(1, LOOPED // 4) as i:
                for q in range(1, 5):
                    slot(4 * i + q, q % XBUFS, True, True, True)
            for n in range(LOOPED + 1, BLOCKS):
                slot(n, n % XBUFS, n + AHEAD < BLOCKS, True, n + 1 < BLOCKS)
            for b in range(BLOCKS - 2, BLOCKS):
                store_rows(b, b % 2)
            for s in range(4, 8):
                for c in range(HC):
                    shared_silu(s, c)
            for t in range(TILES):
                act.wait_ge(combined, t + 1)
                act.wait_ge(z_taken, TILES + t + 1)
                act.dma_start(out[:, t, :], x_all[:, t, :]).then_inc(stored, 16)
            act.wait_ge(stored, 16 * TILES)

        @block.vector
        def _(dve):
            v = nc.vector
            links = [0, 0]
            base = [0]

            def link(ins):
                links[0] += 1
                ins.then_inc(dve_step, 1)
                dve.wait_ge(dve_step, base[0] + links[0])

            def carry():
                v.memset(carrier[:, :], 0.0)

            def norm_var(src, mv, ve, b, done):
                carry()
                link(v.bn_stats(stats[:, b, :], src))
                carry()
                link(v.bn_aggr(mv[:, b, :], stats[:, b, :]))
                v.tensor_scalar(ve[:, b:b + 1], mv[:, b, 1:2], EPS, None, ALU.add).then_inc(done, 1)

            def ln1_stats(j, b):
                norm_var(x_all[:, 2 * j + b, :], mv1, ve1, b, ln1_var)

            def ln1_apply(j, b):
                dve.wait_ge(ln1_rstd, 2 * j + b + 1)
                if not (isinstance(j, int) and j < 1):
                    dve.wait_ge(xnT_ps, j)
                v.tensor_scalar(xn[:, b, :], x_all[:, 2 * j + b, :], mv1[:, b, 0:1], rs1[:, b:b + 1],
                                ALU.subtract, ALU.mult).then_inc(xn_ready, 1)

            def add_attention(j, b):
                n = 2 * j + b
                dve.wait_ge(o_ps, n + 1)
                ins = v.tensor_tensor(att[:, :], work[:, 0:D], bo_bc, ALU.add)
                ins.then_inc(o_taken, 1)
                dve.wait_ge(o_taken, n + 1)
                link(v.scalar_tensor_tensor(out=x_all[:, n, :], in0=att[:, :], scalar=tanh_g[:, 0:1], in1=x_all[:, n, :],
                                            op0=ALU.mult, op1=ALU.add))
                norm_var(x_all[:, n, :], mv2, ve2, b, ln2_var)

            def ln2_apply(j, b):
                n = 2 * j + b
                dve.wait_ge(ln2_rstd, n + 1)
                if not (isinstance(j, int) and j < 1):
                    dve.wait_ge(xf_kept, 2 * j)
                v.tensor_scalar(xfs[:, b, :], x_all[:, n, :], mv2[:, b, 0:1], rs2[:, b:b + 1],
                                ALU.subtract, ALU.mult).then_inc(xf_ready, 1)

            def row_max(j, u):
                n = 4 * j + u
                dve.wait_ge(scores_ready, n + 1)
                link(v.reduce_max(rmax[:, u % 2, :], big[:, u % 2, :, :].rearrange("p a (h k) -> p (a h) k", k=CTX), AX.X))
                v.tensor_scalar(nmax[:, u % 2, :], rmax[:, u % 2, :], -1.0, None, ALU.mult).then_inc(negmax_ready, 1)

            def row_inv(j, u):
                n = 4 * j + u
                dve.wait_ge(exps_done, n + 1)
                if not (isinstance(n, int) and n < 2):
                    dve.wait_ge(probs_ready, n - 1)
                v.reciprocal(rinv[:, u % 2, :], rsum[:, u % 2, :]).then_inc(rinv_ready, 1)

            def copy_xnT(j, bank=work):
                dve.wait_ge(xnT_ps, j + 1)
                if not (isinstance(j, int) and j < 1):
                    dve.wait_ge(q_ps, j)
                v.tensor_copy(xnT.rearrange("p c n -> p (c n)"), bank[:, :]).then_inc(xnT_ready, 1)

            def copy_k(j):
                dve.wait_ge(k_ps, j + 1)
                if not (isinstance(j, int) and j < 1):
                    dve.wait_ge(kblk_ready, 4 * j)
                for m in range(DC):
                    i = v.tensor_scalar(kT[:, m, :], work[:, m * 2 * P:(m + 1) * 2 * P], bias[:, B_K + m:B_K + m + 1], None, ALU.add)
                i.then_inc(kT_ready, 1)

            def copy_q(j, bank=work):
                dve.wait_ge(q_ps, j + 1)
                if not (isinstance(j, int) and j < 1):
                    dve.wait_ge(scores_ready, 4 * j)
                for m in range(DC):
                    i = v.tensor_scalar(qT[:, m, :], bank[:, m * 2 * P:(m + 1) * 2 * P], bias[:, B_Q + m:B_Q + m + 1], SCALE,
                                        ALU.add, ALU.mult)
                i.then_inc(qT_ready, 1)

            def copy_v(j, bank=work):
                dve.wait_ge(v_ps, j + 1)
                if not (isinstance(j, int) and j < 1):
                    dve.wait_ge(v_ready, 4 * j)
                v.tensor_copy(vflat.rearrange("p u c -> p (u c)"), bank[:, :]).then_inc(v_copied, 1)

            def spread_values(j, u):
                dve.wait_ge(v_copied, j + 1)
                if not (isinstance(j, int) and j < 1):
                    dve.wait_ge(av_ready, 4 * j - 3 + u)
                v.tensor_copy(vmask[:, u, :].rearrange("p (h c) -> p h c", h=HG)[:, :, 0:DH],
                              vflat[:, u, :].rearrange("p (h c) -> p h c", h=HG)).then_inc(v_ready, 1)

            def copy_xfT(j):
                dve.wait_ge(xfT_ps, j + 1)
                if not (isinstance(j, int) and j < 1):
                    dve.wait_ge(lg_ps, j)
                    dve.wait_ge(xfT_kept, j)
                v.tensor_copy(xfT[:, :, :].rearrange("p c n -> p (c n)"), work[:, :]).then_inc(xfT_ready, 1)

            def choose_copy(j):
                dve.wait_ge(lg_ps, j + 1)
                v.tensor_copy(logits[:, :, :], work[:, 0:2 * P].rearrange("p (b e) -> p b e", b=2)[:, :, 0:E]) \
                    .then_inc(lg_taken, 1)

            def choose(j):
                dve.wait_ge(lg_taken, j + 1)
                carry()
                for b in range(2):
                    ins = v.max(top8[:, b, :], logits[:, b, :])
                link(ins)
                carry()
                for b in range(2):
                    ins = v.max_index(idx8[:, b, :], top8[:, b, :], logits[:, b, :])
                link(ins)
                link(v.tensor_copy(idxf[:, :, :], idx8[:, :, 0:TOPK]))
                for b in range(2):
                    for k in range(TOPK):
                        v.tensor_scalar(chosen[:, k, 2 * j + b, :], const[:, C_IE:C_IE + E], idxf[:, b, k:k + 1], None, ALU.is_equal)
                        ins = v.tensor_copy(top2[:, k, bass.ds(2 * j + b, 1)], top8[:, b, k:k + 1])
                link(ins)

            def pair(j, ahead, behind, ahead2):
                for u in range(UNITS):
                    if u < UNITS - 1:
                        row_inv(j, u + 1)
                    elif ahead:
                        row_inv(j + 1, 0)
                    if u == 0 and not (isinstance(j, int) and j < 1):
                        spread_values(j, UNITS - 1)
                    if u == 3 and ahead:
                        for w in range(UNITS - 1):
                            spread_values(j + 1, w)
                    if behind and u < 2:
                        add_attention(j - 1, u)
                    if behind and u == 2:
                        copy_xfT(j - 1)
                    if behind and u == 3:
                        choose_copy(j - 1)
                    if u < 2:
                        row_max(j, u + 2)
                    elif ahead:
                        row_max(j + 1, u - 2)
                    if ahead2 and u == 2:
                        for b in range(2):
                            ln1_stats(j + 2, b)
                    if ahead and u < 3:
                        (copy_k, copy_q, copy_v)[u](j + 1)
                    if ahead2 and u == 3:
                        copy_xnT(j + 2)
                    if behind and u < 2:
                        ln2_apply(j - 1, u)
                    if ahead2 and u == 2:
                        for b in range(2):
                            ln1_apply(j + 2, b)
                    if behind and u == 3:
                        choose(j - 1)

            v.memset(mhalf[:, :], -0.5).then_inc(half_ready, 1)
            v.memset(wg_pad[:, :, :], 0.0).then_inc(wg_zero, 1)
            dve.wait_ge(x_head_loaded, 16)
            for b in range(2):
                ln1_stats(0, b)
            for b in range(2):
                ln1_apply(0, b)
            copy_xnT(0, mid[:, 0, :])
            dve.wait_ge(x_next_loaded, 16)
            for b in range(2):
                ln1_stats(1, b)
            dve.wait_ge(bias_loaded, 16)
            copy_k(0)
            copy_q(0, last)
            for b in range(2):
                ln1_apply(1, b)
            copy_v(0, mid[:, 1, :])
            copy_xnT(1)
            row_max(0, 0)
            row_max(0, 1)
            dve.wait_ge(vmask_zero, 1)
            for u in range(UNITS):
                spread_values(0, u)
            row_inv(0, 0)
            dve.wait_ge(x_loaded, 16)
            dve.wait_ge(bo_loaded, 16)
            dve.wait_ge(tanh_ready, 1)
            pair(0, True, False, True)
            pair(1, True, True, True)
            before = links[0]
            LINKS = UNITS + 2 * 3 + 2 * 2 + 4
            with dve.Fori(2, LAST - 1) as j:
                base[0] = (j - 2) * LINKS
                pair(j, True, True, True)
            assert links[0] - before == LINKS, links[0] - before
            base[0] = (LAST - 4) * LINKS
            pair(LAST - 1, True, True, False)
            pair(LAST, False, True, False)
            def copy_rows(b, p):
                dve.wait_ge(xs_ps, b + 1)
                if not (isinstance(b, int) and b < 2):
                    dve.wait_ge(up_ps, b - 1)
                v.tensor_copy(xsT_hi[:, p, :], work[:, 0:D]).then_inc(rows_hi, 1)
                dve.wait_ge(rows_hi, b + 1)
                v.tensor_tensor(xsT_lo[:, p, :], work[:, 0:D], xsT_hi[:, p, :], ALU.subtract).then_inc(xsT_ready, 1)

            def shared_hidden(s, chunks):
                for c in chunks:
                    n = HC * s + c
                    o = B_S11 + HC * (s // (TILES // GROUP)) + c
                    dve.wait_ge(silu_ready, n + 1)
                    if s >= 2:
                        dve.wait_ge(z_ps, GROUP * (s - 1))
                    v.scalar_tensor_tensor(out=gshT[:, s % 2, c, :], in0=big[:, c % 2, 1, :], scalar=bias[:, o:o + 1],
                                           in1=sil[:, c % 2, :], op0=ALU.add, op1=ALU.mult).then_inc(gsh_ready, 1)

            def add_shared(s, tiles=range(GROUP)):
                h, g = divmod(s, TILES // GROUP)
                for t in tiles:
                    n = GROUP * s + t
                    tile = GROUP * g + t
                    dve.wait_ge(z_ps, n + 1)
                    if h == 0:
                        v.tensor_tensor(zt, zbank[t % 2][:, 0:D], bs2_bc[:, :], ALU.add).then_inc(z_taken, 1)
                        dve.wait_ge(z_taken, n + 1)
                        v.scalar_tensor_tensor(out=x_all[:, tile, :], in0=zt, scalar=tanh_g[:, 1:2], in1=x_all[:, tile, :],
                                               op0=ALU.mult, op1=ALU.add).then_inc(z_added, 1)
                        dve.wait_ge(z_added, n + 1)
                    else:
                        if g > 0:
                            dve.wait_ge(combined, GATHERS if g == 1 else TILES)
                        v.scalar_tensor_tensor(out=x_all[:, tile, :], in0=zbank[t % 2][:, 0:D], scalar=tanh_g[:, 1:2],
                                               in1=x_all[:, tile, :], op0=ALU.mult, op1=ALU.add).then_inc(z_taken, 1)
                        dve.wait_ge(z_taken, n + 1)

            for b in range(2):
                add_attention(LAST, b)
                ln2_apply(LAST, b)
                shared_hidden(0, [b])
            copy_xfT(LAST)
            shared_hidden(0, [2])
            choose_copy(LAST)
            choose(LAST)

            def r3(i):
                return rt[:, i, :].rearrange("p (t e) -> p t e", t=TILES)

            ins = v.tensor_tensor(r3(0), chosen[:, 0, :, :], chosen[:, 1, :, :], ALU.add)
            ins.then_inc(onehots_ready, 1)
            v.tensor_tensor(gtmp[:, 0, :], top2[:, 1, :], top2[:, 0, :], ALU.subtract).then_inc(gate_exp_in, 1)
            shared_hidden(0, [3])
            shared_hidden(1, [0])
            dve.wait_ge(rank_ps, 1)
            link(v.tensor_copy(rt[:, 1, :], mid[:, 1, 0:TILES * E]))
            cur, nxt, step = 1, 2, 1
            while step < TILES:
                v.tensor_copy(r3(nxt)[:, 0:step, :], r3(cur)[:, 0:step, :])
                link(v.tensor_tensor(r3(nxt)[:, step:, :], r3(cur)[:, step:, :], r3(cur)[:, :TILES - step, :], ALU.add))
                cur, nxt = nxt, 3 if nxt == 2 else 2
                step *= 2
            shared_hidden(1, [1])
            total = r3(cur)[:, TILES - 1, :]
            other = 2 if cur == 3 else 3
            cmp16 = blk_cmp[:, 0:TILES, :]
            link(v.tensor_tensor(cmp16, total.unsqueeze(1).to_broadcast([P, TILES, E]),
                                 const[:, C_IT:C_IT + TILES].unsqueeze(2).to_broadcast([P, TILES, E]), ALU.is_gt))
            link(v.tensor_reduce(cnt[:, 5, :], cmp16.rearrange("p t e -> p e t"), AX.X, ALU.add))
            link(v.tensor_scalar(cnt[:, 0, :], cnt[:, 5, :], 1.0, None, ALU.max))
            c_cur, c_nxt, step = 0, 1, 1
            while step < E:
                v.tensor_copy(cnt[:, c_nxt, 0:step], cnt[:, c_cur, 0:step])
                link(v.tensor_tensor(cnt[:, c_nxt, step:], cnt[:, c_cur, step:], cnt[:, c_cur, :E - step], ALU.add))
                c_cur, c_nxt = c_nxt, c_nxt + 1
                step *= 2
            ends = cnt[:, c_cur, :]
            v.tensor_copy(blk_end[:, :], ends)
            link(v.tensor_tensor(blk_cmp[:, :, :], ends.unsqueeze(1).to_broadcast([P, BLOCKS, E]),
                                 const[:, C_IB:C_IB + BLOCKS].unsqueeze(2).to_broadcast([P, BLOCKS, E]), ALU.is_le))
            link(v.tensor_reduce(blk_f[:, :], blk_cmp[:, :, :], AX.X, ALU.add))
            v.tensor_scalar(blk_item[:, :], blk_f[:, :], float(E - 1), 1.0, ALU.min, ALU.add).then_inc(table_ready, 1)
            link(v.tensor_tensor(cnt[:, 5, :], ends, cnt[:, 0, :], ALU.subtract))
            link(v.tensor_tensor(r3(other), r3(cur), r3(1), ALU.subtract))
            link(v.scalar_tensor_tensor(out=r3(cur), in0=cnt[:, 5, :].unsqueeze(1).to_broadcast([P, TILES, E]), scalar=float(P),
                                        in1=r3(other), op0=ALU.mult, op1=ALU.add))
            ins = v.tensor_tensor(r3(other), r3(cur), mid[:, 0, 0:TILES * E].rearrange("p (t e) -> p t e", t=TILES), ALU.add)
            ins.then_inc(rank_taken, 1)
            dve.wait_ge(rank_taken, 1)
            for k in range(TOPK):
                link(v.tensor_tensor(r3(0), chosen[:, k, :, :], r3(other), ALU.mult))
                link(v.tensor_reduce(pos_f[:, k, :], r3(0), AX.X, ALU.add))
            v.tensor_copy(pos[:, :, :], pos_f[:, :, :]).then_inc(pos_ready, 1)
            shared_hidden(1, [2, 3])
            dve.wait_ge(w_even, 32)
            add_shared(0)
            shared_hidden(2, range(HC))
            add_shared(1)
            shared_hidden(3, range(HC))
            add_shared(2)
            copy_rows(0, 0)
            add_shared(3, range(1))
            copy_rows(1, 1)
            dve.wait_ge(gate_exp, 1)
            link(v.tensor_scalar(gtmp[:, 2, :], gtmp[:, 1, :], 1.0, None, ALU.add))
            link(v.reciprocal(gtmp[:, 0, :], gtmp[:, 2, :]))
            link(v.tensor_scalar(gate[:, 0, :], gtmp[:, 0, :], tanh_g[:, 1:2], None, ALU.mult))
            v.tensor_tensor(gate[:, 1, :], gate[:, 0, :], gtmp[:, 1, :], ALU.mult).then_inc(gates_ready, 1)

            def slot_of(b):
                item = dve.value_load(blk_item[0:1, bass.ds(b, 1)], min_val=1, max_val=E)
                return dve.snap(item % WSLOTS)

            def add_biases(b, p):
                slot = slot_of(b)
                dve.wait_ge(up_ps, b + 1)
                if not (isinstance(b, int) and b < 2):
                    dve.wait_ge(s_ready, b - 1)
                    dve.wait_ge(g_ready, b - 1)
                v.tensor_tensor(hb1[:, p, :], big[:, p, 0, :], bring[:, slot, 0:HID], ALU.add).then_inc(h1_ready, 1)
                v.tensor_tensor(hb11[:, p, :], big[:, p, 1, :], bring[:, slot, HID:2 * HID], ALU.add).then_inc(h_taken, 1)

            def hidden(b, p):
                dve.wait_ge(s_ready, b + 1)
                dve.wait_ge(h_taken, b + 1)
                if not (isinstance(b, int) and b < 2):
                    dve.wait_ge(gt_ps, b - 1)
                v.tensor_tensor(gg[:, p, :], sl[:, p, :], hb11[:, p, :], ALU.mult).then_inc(g_ready, 1)

            def add_out_bias(b, p):
                slot = slot_of(b)
                dve.wait_ge(down_ps, b + 1)
                if not (isinstance(b, int) and b < 2):
                    dve.wait_ge(y_st_odd if p else y_st_even, 8 * (b - p))
                v.tensor_tensor(ysb[:, p, :], mid[:, 1, 0:D], bring[:, slot, 2 * HID:BCOLS], ALU.add).then_inc(y_ready, 1)

            dve.wait_ge(table_ready, 1)
            def slot(n, q, rows, ahead):
                p = q % 2
                if ahead:
                    add_biases(n + 1, 1 - p)
                if rows:
                    copy_rows(n + 3, 1 - p)
                if ahead:
                    hidden(n + 1, 1 - p)
                add_out_bias(n - 1, 1 - p)

            add_biases(0, 0)
            add_shared(3, range(1, GROUP))
            copy_rows(2, 0)
            hidden(0, 0)
            add_biases(1, 1)
            copy_rows(3, 1)
            hidden(1, 1)
            for n in range(1, 5):
                slot(n, n % XBUFS, True, True)
            with dve.Fori(1, LOOPED // 4) as i:
                for q in range(1, 5):
                    slot(4 * i + q, q % XBUFS, True, True)
            for n in range(LOOPED + 1, BLOCKS):
                slot(n, n % XBUFS, n + 3 < BLOCKS, n + 1 < BLOCKS)
            add_out_bias(BLOCKS - 1, (BLOCKS - 1) % 2)

            def combine(t):
                n, yg = t % GATHERS, yg_b if t >= GATHERS else yg_a
                dve.wait_ge(gathered_b if t >= GATHERS else gathered, 32 * GATHERS)
                link(v.scalar_tensor_tensor(out=x_all[:, t, :], in0=yg[:, n, 0, :], scalar=gate[:, 0, t:t + 1], in1=x_all[:, t, :],
                                            op0=ALU.mult, op1=ALU.add))
                v.scalar_tensor_tensor(out=x_all[:, t, :], in0=yg[:, n, 1, :], scalar=gate[:, 1, t:t + 1], in1=x_all[:, t, :],
                                       op0=ALU.mult, op1=ALU.add).then_inc(combined, 1)

            dve.wait_ge(gates_ready, 1)
            shared_hidden(4, range(HC))
            shared_hidden(5, range(HC))
            add_shared(4)
            for c in range(HC):
                shared_hidden(6, [c])
                combine(2 * c)
                combine(2 * c + 1)
            add_shared(5)
            for c in range(HC):
                shared_hidden(7, [c])
                combine(GATHERS + 2 * c)
                combine(GATHERS + 2 * c + 1)
            add_shared(6)
            add_shared(7)

        @block.gpsimd
        def _(pool):
            g = nc.gpsimd

            def rstd1(j, b):
                pool.wait_ge(ln1_var, 2 * j + b + 1)
                if not (isinstance(j, int) and j < 1):
                    pool.wait_ge(xn_ready, 2 * j)
                g.tensor_tensor(rs1[:, b:b + 1], ve1[:, b:b + 1], mhalf[:, :], ALU.pow).then_inc(ln1_rstd, 1)

            def rstd2(j, b):
                pool.wait_ge(ln2_var, 2 * j + b + 1)
                if not (isinstance(j, int) and j < 1):
                    pool.wait_ge(xf_ready, 2 * j)
                g.tensor_tensor(rs2[:, b:b + 1], ve2[:, b:b + 1], mhalf[:, :], ALU.pow).then_inc(ln2_rstd, 1)

            def spread_keys(j, u):
                b, m = divmod(u, 2)
                n = 4 * j + u
                if u == 0:
                    pool.wait_ge(kT_ready, j + 1)
                if not (isinstance(n, int) and n < 2):
                    pool.wait_ge(scores_ready, n - 1)
                g.tensor_tensor(kblk[:, u % 2, :, :],
                                kT[:, m, b * CTX:(b + 1) * CTX].unsqueeze(1).to_broadcast([P, HG, CTX]),
                                const[:, C_HM:C_HM + HG].unsqueeze(2).to_broadcast([P, HG, CTX]), ALU.mult) \
                    .then_inc(kblk_ready, 1)

            def normalise(j, u):
                n = 4 * j + u
                pool.wait_ge(rinv_ready, n + 1)
                g.tensor_tensor(probs[:, u % 2, :, :], probs[:, u % 2, :, :],
                                rinv[:, u % 2, :].unsqueeze(2).to_broadcast([P, HG, CTX]), ALU.mult).then_inc(probs_ready, 1)

            def keep_xf(j, b):
                pool.wait_ge(xf_ready, 2 * j + b + 1)
                g.tensor_copy(xf_all[:, 2 * j + b, :], xfs[:, b, :]).then_inc(xf_kept, 1)

            def keep_xfT(j):
                pool.wait_ge(xfT_ready, j + 1)
                part = bass.ds(2 * P * j, 2 * P)
                g.tensor_tensor(xfT_hi[:, :, part], xfT[:, :, :], const[:, C_ONE:C_ONE + 1].unsqueeze(2).to_broadcast([P, DC, 2 * P]),
                                ALU.mult).then_inc(xfT_hi_kept, 1)
                pool.wait_ge(xfT_hi_kept, j + 1)
                g.tensor_tensor(xfT_lo[:, :, part], xfT[:, :, :], xfT_hi[:, :, part], ALU.subtract).then_inc(xfT_kept, 1)

            def split(before, source, slot, part, parts):
                n = slice(part * UCOLS // parts, (part + 1) * UCOLS // parts)
                ones = const[:, C_ONE:C_ONE + 1].to_broadcast([P, UCOLS // parts])
                g.tensor_tensor(u_hi[:, slot, n], source[:, n], ones, ALU.mult).then_inc(hi_done, 1)
                pool.wait_ge(hi_done, before + 1)
                ins = g.tensor_tensor(u_lo[:, slot, n], source[:, n], u_hi[:, slot, n], ALU.subtract)
                if part == parts - 1:
                    ins.then_inc(split_done, 1)

            def pair(j, ahead, behind, ahead2, split_first):
                for u in range(UNITS):
                    if u < UNITS - 1:
                        normalise(j, u + 1)
                    elif ahead:
                        normalise(j + 1, 0)
                    if u == 0:
                        spread_keys(j, UNITS - 1)
                    elif ahead:
                        spread_keys(j + 1, u - 1)
                    if behind and u < 2:
                        rstd2(j - 1, u)
                    if ahead2 and u == 2:
                        for b in range(2):
                            rstd1(j + 2, b)
                    if behind and u in (1, 2):
                        keep_xf(j - 1, u - 1)
                    if behind and u == 3:
                        keep_xfT(j - 1)
                    if split_first:
                        pool.wait_ge(raw_first_loaded, 16)
                        split(u, raw_first, 0, u, UNITS)

            pool.wait_ge(half_ready, 1)
            g.memset(vmask, 0.0).then_inc(vmask_zero, 1)
            for b in range(2):
                rstd1(0, b)
            for b in range(2):
                rstd1(1, b)
            pool.wait_ge(const_loaded, 16)
            spread_keys(0, 0)
            spread_keys(0, 1)
            g.memset(dring[:, :, :], 0.0).then_inc(xs_zero, 1)
            spread_keys(0, 2)
            normalise(0, 0)
            pair(0, True, False, True, False)
            pair(1, True, True, True, False)
            with pool.Fori(2, LAST - 1) as j:
                pair(j, True, True, True, False)
            pair(LAST - 1, True, True, False, True)
            pair(LAST, False, True, False, False)

            for b in range(2):
                rstd2(LAST, b)
            for b in range(2):
                keep_xf(LAST, b)
            keep_xfT(LAST)

            pool.wait_ge(raw_odd, 16)
            split(UNITS, raw[:, 1, :], 1, 0, 1)

            pool.wait_ge(pos_ready, 1)
            pool.wait_ge(xf_kept, TILES)
            pool.wait_ge(zeroed, 16 * ZDMAS)
            for t in range(TILES):
                for k in range(TOPK):
                    g.indirect_dma_start(out=sorted_x, out_offset=bass.IndirectOffsetOnAxis(ap=pos[:, k, t:t + 1], axis=0),
                                         in_=xf_all[:, t, :], in_offset=None).then_inc(scattered, 16)

            pool.wait_ge(raw_even, 16)
            pool.wait_ge(sh_ps, HC * TILES // GROUP)
            split(UNITS + 1, raw[:, 0, :], 0, 0, 1)
            pool.wait_ge(table_ready, 1)

            def split_expert(i, slot):
                pool.wait_ge(raw_odd if slot else raw_even, 8 * i + (8 if slot else 0))
                end = pool.value_load(blk_end[0:1, bass.ds(i - USLOTS - 1, 1)], min_val=1, max_val=BLOCKS)
                pool.wait_ge(up_ps, end)
                split(UNITS + i - 1, raw[:, slot, :], slot, 0, 1)

            with pool.Fori(0, (E - 2) // 2) as i:
                split_expert(2 * i + 3, 1)
                split_expert(2 * i + 4, 0)
            split_expert(ITEMS - 1, 1)
            pool.wait_ge(y_st_even, 16 * ((BLOCKS + 1) // 2))
            pool.wait_ge(y_st_odd, 16 * (BLOCKS // 2))
            for t in range(TILES):
                yg = yg_b if t >= GATHERS else yg_a
                for k in range(TOPK):
                    g.indirect_dma_start(out=yg[:, t % GATHERS, k, :], out_offset=None, in_=sorted_y,
                                         in_offset=bass.IndirectOffsetOnAxis(ap=pos[:, k, t:t + 1], axis=0)) \
                        .then_inc(gathered_b if t >= GATHERS else gathered, 16)


def kernel(x, ctx_1024, g_xattn, g_ffn, L0_xattn_Wq, L0_xattn_bq, L0_xattn_Wk, L0_xattn_bk, L0_xattn_Wv, L0_xattn_bv,
           L0_xattn_Wo, L0_xattn_bo, L0_ffn_Wg, L0_ffn_W1, L0_ffn_b1, L0_ffn_W11, L0_ffn_b11, L0_ffn_W2, L0_ffn_b2,
           L0_ffn_Ws1, L0_ffn_bs1, L0_ffn_Ws11, L0_ffn_bs11, L0_ffn_Ws2, L0_ffn_bs2):
    import numpy as np
    import concourse.bacc as bacc
    from concourse.bass_utils import run_bass_kernel_spmd

    def rows(w):
        w = np.asarray(w)
        return w.reshape(w.shape[0] // P, P, w.shape[1]).transpose(1, 0, 2)

    def cols(v):
        return np.asarray(v).reshape(-1, P).T

    attn_w = np.stack([rows(np.asarray(w).T) for w in (L0_xattn_Wq, L0_xattn_Wk, L0_xattn_Wv, L0_xattn_Wo)], axis=1)
    col_bias = np.concatenate([cols(v) for v in (L0_xattn_bq, L0_xattn_bk, L0_xattn_bv, L0_ffn_bs1, L0_ffn_bs11)], axis=1)

    def expert_rows(w):
        w = np.asarray(w)
        return w.reshape(E, w.shape[1] // P, P, w.shape[2]).transpose(0, 2, 1, 3).reshape(E, P, -1)

    expert_up = np.concatenate([expert_rows(w) for w in (L0_ffn_W1, L0_ffn_W11)], axis=2)
    halves = [slice(h * HID, (h + 1) * HID) for h in range(HALVES)]
    half_up = [np.concatenate([rows(np.asarray(w)[:, h]).reshape(P, -1) for w in (L0_ffn_Ws1, L0_ffn_Ws11)], axis=1) for h in halves]
    half_down = [rows(np.asarray(L0_ffn_Ws2)[h]).reshape(P, -1) for h in halves]
    up_w = np.concatenate([half_up[0][None], expert_up, half_up[1][None]])
    down_w = np.concatenate([half_down[0][None], expert_rows(L0_ffn_W2), half_down[1][None]])
    expert_bias = np.concatenate([np.asarray(b) for b in (L0_ffn_b1, L0_ffn_b11, L0_ffn_b2)], axis=1)
    i = np.arange(P)
    consts = np.zeros((P, CONSTS), np.float32)
    consts[:, C_ID:C_ID + P] = np.eye(P)
    consts[:, C_TRI:C_TRI + P] = i[:, None] < i[None, :]
    consts[:, C_ONE:C_ONE + P] = 1
    consts[:, C_HM:C_HM + HG] = i[:, None] // DH == np.arange(HG)[None, :]
    consts[:, C_IE:C_IE + E] = np.arange(E)
    consts[:, C_IB:C_IB + BLOCKS] = np.arange(BLOCKS)
    consts[:, C_IT:C_IT + TILES] = np.arange(TILES) * P

    ins = {
        "x": np.asarray(x).transpose(1, 0, 2),
        "ctx_t": np.asarray(ctx_1024).reshape(PAIRS, 2 * CTX, DC, P).transpose(0, 3, 2, 1),
        "attn_w": attn_w, "col_bias": col_bias, "bo": np.asarray(L0_xattn_bo),
        "g_xattn": np.asarray(g_xattn), "g_ffn": np.asarray(g_ffn), "w_gate": rows(L0_ffn_Wg),
        "up_w": up_w, "down_w": down_w, "expert_bias": expert_bias, "bs2": np.asarray(L0_ffn_bs2),
        "consts": consts,
    }
    nc = bacc.Bacc("TRN2", target_bir_lowering=False, num_devices=1)
    arrays, args = {}, []
    for name, a in ins.items():
        arrays[f"{name}_dram"] = a = np.ascontiguousarray(a)
        args.append(nc.dram_tensor(f"{name}_dram", a.shape, mybir.dt.from_np(a.dtype), kind="ExternalInput").ap())
    args.append(nc.dram_tensor("out_dram", (P, TILES, D), F32, kind="ExternalOutput").ap())
    flamingo_layer(nc, *args)
    r = run_bass_kernel_spmd(nc, [arrays], core_ids=[0])
    return np.ascontiguousarray(r.results[0]["out_dram"].transpose(1, 0, 2))
```
